# Optimizing a Trainium2 kernel written in Bass

```python
import numpy as np
import jax
import jax.numpy as jnp

def _softmax(x, axis=-1):
    return jax.nn.softmax(x, axis=axis)

def _gelu(x):
    return jax.nn.gelu(x, approximate=True)

def _silu(x):
    return jax.nn.silu(x)

def _sigmoid(x):
    return jax.nn.sigmoid(x)

def _layernorm(x, axis=-1, eps=1e-05):
    m = jnp.mean(x, axis=axis, keepdims=True)
    v = jnp.var(x, axis=axis, keepdims=True)
    return (x - m) / jnp.sqrt(v + eps)

def _scatter_add(tgt, idx, src, axis=0):
    return tgt.at[idx].add(src)

def _segment_sum(src, seg, n):
    return jax.ops.segment_sum(src, seg, n)
kernel_name = 'mk_recurrent_d1_jaxref_r4_ee35cf'

def setup_inputs(seed: int=0):
    np.random.seed(seed)
    _w = jnp.asarray

    def _L0_attn_setup():
        import jax, jax.numpy as jnp
        import numpy as np
        N_HEADS = 16
        ROPE_BASE = 10000.0

        def _rope(x):
            B, L, H, Dh = x.shape
            half = Dh // 2
            inv_freq = 1.0 / ROPE_BASE ** (jnp.arange(0, half, dtype=jnp.float32) / half)
            ang = jnp.arange(L, dtype=jnp.float32)[:, None] * inv_freq[None, :]
            cos = jnp.concatenate([jnp.cos(ang), jnp.cos(ang)], axis=-1).astype(x.dtype)
            sin = jnp.concatenate([jnp.sin(ang), jnp.sin(ang)], axis=-1).astype(x.dtype)
            cos = cos[None, :, None, :]
            sin = sin[None, :, None, :]
            x1, x2 = (x[..., :half], x[..., half:])
            rot = jnp.concatenate([-x2, x1], axis=-1)
            return x * cos + rot * sin
        key = jax.random.key(seed)
        k1, k2, k3 = jax.random.split(key, 3)
        B, L, D = (2, 512, 256)
        x = jax.random.normal(k1, (B, L, D), dtype=jnp.float32)
        w_qkv = jax.random.normal(k2, (3 * D, D), dtype=jnp.float32) * D ** (-0.5)
        w_out = jax.random.normal(k3, (D, D), dtype=jnp.float32) * D ** (-0.5)
        return {'x': x, 'w_qkv': w_qkv, 'w_out': w_out}
    _L0_attn_in = _L0_attn_setup()

    def _L0_ffn_setup():
        import jax, jax.numpy as jnp
        import numpy as np
        B, S, H, E, D = (4, 1024, 256, 8, 64)
        key = jax.random.key(seed)
        k0, k1, k2, k3, k4 = jax.random.split(key, 5)
        scale_h = 1.0 / np.sqrt(H)
        scale_d = 1.0 / np.sqrt(D)
        return {'x': jax.random.normal(k0, (B, S, H), dtype=jnp.float32), 'gate_w': jax.random.normal(k1, (E, H), dtype=jnp.float32) * scale_h, 'wg': jax.random.normal(k2, (E, H, D), dtype=jnp.float32) * scale_h, 'wu': jax.random.normal(k3, (E, H, D), dtype=jnp.float32) * scale_h, 'wd': jax.random.normal(k4, (E, D, H), dtype=jnp.float32) * scale_d}
    _L0_ffn_in = _L0_ffn_setup()
    _d = {'L0_attn_x': _L0_attn_in['x'], 'L0_attn_w_qkv': _L0_attn_in['w_qkv'], 'L0_attn_w_out': _L0_attn_in['w_out'], 'L0_ffn_gate_w': _L0_ffn_in['gate_w'], 'L0_ffn_wg': _L0_ffn_in['wg'], 'L0_ffn_wu': _L0_ffn_in['wu'], 'L0_ffn_wd': _L0_ffn_in['wd']}
    _x0 = _d['L0_attn_x']
    _d['L0_attn_x'] = jax.random.normal(jax.random.fold_in(jax.random.key(seed), 1), (2, 2048, 256), dtype=_x0.dtype)
    del _x0
    return _d

def reference(L0_attn_x, L0_attn_w_qkv, L0_attn_w_out, L0_ffn_gate_w, L0_ffn_wg, L0_ffn_wu, L0_ffn_wd):

    def _L0_attn_ref(x, w_qkv, w_out):
        import jax, jax.numpy as jnp
        import numpy as np
        N_HEADS = 16
        ROPE_BASE = 10000.0

        def _rope(x):
            B, L, H, Dh = x.shape
            half = Dh // 2
            inv_freq = 1.0 / ROPE_BASE ** (jnp.arange(0, half, dtype=jnp.float32) / half)
            ang = jnp.arange(L, dtype=jnp.float32)[:, None] * inv_freq[None, :]
            cos = jnp.concatenate([jnp.cos(ang), jnp.cos(ang)], axis=-1).astype(x.dtype)
            sin = jnp.concatenate([jnp.sin(ang), jnp.sin(ang)], axis=-1).astype(x.dtype)
            cos = cos[None, :, None, :]
            sin = sin[None, :, None, :]
            x1, x2 = (x[..., :half], x[..., half:])
            rot = jnp.concatenate([-x2, x1], axis=-1)
            return x * cos + rot * sin
        B, L, D = x.shape
        H = N_HEADS
        Dh = D // H
        qkv = jnp.einsum('bld,ed->ble', x, w_qkv)
        q, k, v = jnp.split(qkv, 3, axis=-1)
        q = q.reshape(B, L, H, Dh)
        k = k.reshape(B, L, H, Dh)
        v = v.reshape(B, L, H, Dh)
        q = _rope(q)
        k = _rope(k)
        scale = 1.0 / jnp.sqrt(jnp.asarray(Dh, dtype=x.dtype))
        scores = jnp.einsum('blhd,bmhd->bhlm', q, k) * scale
        attn = jax.nn.softmax(scores, axis=-1)
        out = jnp.einsum('bhlm,bmhd->blhd', attn, v).reshape(B, L, D)
        return jnp.einsum('bld,ed->ble', out, w_out)

    def _L0_ffn_ref(x, gate_w, wg, wu, wd):
        import jax, jax.numpy as jnp
        import numpy as np
        B, S, H, E, D = (4, 1024, 256, 8, 64)
        b, s, h = x.shape
        xf = x.reshape(-1, h)
        logits = jnp.einsum('th,eh->te', xf, gate_w)
        expert_idx = jnp.argmax(logits, axis=-1)
        onehot = jax.nn.one_hot(expert_idx, gate_w.shape[0], dtype=x.dtype)
        g = jnp.einsum('th,ehd->etd', xf, wg)
        u = jnp.einsum('th,ehd->etd', xf, wu)
        inter = jnp.square(jax.nn.relu(g)) * u
        inter = inter * onehot.T[:, :, None]
        out = jnp.einsum('etd,edh->th', inter, wd)
        return out.reshape(b, s, h)
    x = L0_attn_x
    xn = _layernorm(x, axis=-1)
    s = _L0_attn_ref(xn, L0_attn_w_qkv, L0_attn_w_out)
    g = _silu(_L0_ffn_ref(xn, L0_ffn_gate_w, L0_ffn_wg, L0_ffn_wu, L0_ffn_wd))
    x = x + s * g
    return x

_drawn_inputs = setup_inputs


def setup_inputs(seed=0):
    import zlib

    import numpy as np

    out = dict(_drawn_inputs(seed))
    spreads = {}
    factors = {}
    for name, (base, spread) in spreads.items():
        noise = np.random.default_rng([zlib.crc32(name.encode()), seed]).standard_normal(out[name].shape)
        drawn = base * np.exp(spread * noise) if base else spread * noise
        out[name] = jnp.asarray(drawn.astype(out[name].dtype))
    for name, factor in factors.items():
        out[name] = (out[name] * factor).astype(out[name].dtype)
    return out
```

```python
import concourse.bass as bass
from concourse import mybir
from contextlib import ExitStack


def layer_kernel(nc, x_in, w_in, wout_in, wg_in, wu_in, wd_in, rope_in, ident_in, rank_in, out):
    F32, BF16 = mybir.dt.float32, mybir.dt.bfloat16
    ALU, ACT, AX = mybir.AluOpType, mybir.ActivationFunctionType, mybir.AxisListType

    B, L, D = 2, 2048, 256
    H, DH = 16, 16
    E, DE = 8, 64
    P = 128
    NT = B * L // P
    GT = 4
    NG = NT // GT
    W = GT * P
    KC = D // P
    NX = 4
    EC = E * DE // P
    QK = 2 * D
    VG = D + E
    NPART = 3
    QPARTS = (0, 0, 0, 1, 1, 1, 2)
    KPARTS = (0, 1, 2, 0, 1, 2, 0)
    KR = DH * len(QPARTS)
    KS = KR + NPART
    NM = NPART * 2 * KC
    HM = NM // 2
    NH = B * H
    KB = L // P
    QT = L // W
    SCALE = DH ** -0.5
    EPS = 1e-5
    STORES = QT + 1
    LOADS = 7

    x_v = x_in.rearrange("b (t p) d -> p (b t) d", p=P)
    out_v = out.rearrange("b (t p) d -> p (b t) d", p=P)

    ctx = ExitStack()
    with ctx:
        def sb(name, shape, dt=F32):
            return ctx.enter_context(nc.sbuf_tensor(name, shape, dt))

        def sem(name):
            return ctx.enter_context(nc.semaphore(name))

        parts_d = nc.dram_tensor("parts_d", (NPART, 2, D, B * L), BF16, kind="Internal").ap()
        shift_d = nc.dram_tensor("shift_d", (NPART, NH * L), BF16, kind="Internal").ap()
        onum_d = nc.dram_tensor("onum_d", (B, D, L), F32, kind="Internal").ap()
        orec_d = nc.dram_tensor("orec_d", (B, H, L), F32, kind="Internal").ap()

        x_sb = sb("x_sb", [P, NT, D])
        v_sb = sb("v_sb", [P, NT, D])
        gate = sb("gate", [P, NT, D])
        w_sb = sb("w_sb", [P, KC, QK + VG])
        wg_sb = sb("wg_sb", [P, KC, E * DE])
        wu_sb = sb("wu_sb", [P, KC, E * DE])
        wd_sb = sb("wd_sb", [P, EC, D])
        wo_sb = sb("wo_sb", [P, KC, D])
        rope = sb("rope", [P, NT, 3 * DH // 2])
        ident = sb("ident", [P, P])
        ident_b = sb("ident_b", [P, P], BF16)
        rank = sb("rank", [P, E])
        stats = sb("stats", [P, NT, 6])
        mean = sb("mean", [P, NT])
        rstd = sb("rstd", [P, NT])
        tmp = sb("tmp", [P, 4, NT])
        negm = sb("negm", [P, NH * KB])

        ARENA = 21504
        arena = sb("arena", [P, ARENA])
        at = [0]

        def cut(shape, dt=F32):
            n = 1
            for s in shape:
                n *= s
            words = n * (2 if dt == BF16 else 4) // 4
            flat = arena[:, at[0]:at[0] + words]
            at[0] += words
            assert at[0] <= ARENA
            if dt == BF16:
                flat = flat.bitcast(BF16)
            if len(shape) == 1:
                return flat
            names = "abcd"[:len(shape)]
            return flat.rearrange(f"p ({' '.join(names)}) -> p {' '.join(names)}", **dict(zip(names, shape)))

        xn = [cut([GT, D]) for _ in range(2)]
        xnT = [cut([KC, W]) for _ in range(2)]
        qk_s = [cut([QK]) for _ in range(GT)]
        qk_q = [cut([QK], BF16) for _ in range(GT)]
        ra, rb, rq = cut([QK]), cut([QK]), cut([QK])
        parts = [cut([NPART, QK], BF16) for _ in range(2)]
        pst = cut([NM, W], BF16)
        hid = [cut([W]) for _ in range(2)]
        hid_m = [cut([W]) for _ in range(2)]
        hid_q = [cut([W]) for _ in range(2)]
        inter = cut([EC, W])
        ey = [cut([2, D]) for _ in range(2)]
        choice = cut([GT, E, DE], BF16)
        logit = cut([GT, E])
        hit = cut([GT, E])
        won = cut([GT, E])
        best = cut([GT])
        assert at[0] <= ARENA
        at[0] = 0
        qst = [cut([L], BF16) for _ in range(2)]
        kst = [cut([L], BF16) for _ in range(2)]
        prob = [cut([L]) for _ in range(2)]
        vst = [cut([KB, 32]) for _ in range(2)]
        osb = [cut([W]) for _ in range(2)]
        orc = [cut([W]) for _ in range(2)]
        mpart = cut([NPART, NH * KB], BF16)
        mres = cut([NH * KB])
        mrow = cut([NPART, NH * KB], BF16)
        at[0] = 0
        onum = cut([KC, L])
        orec = cut([KC, L])
        res = [cut([2, D]) for _ in range(2)]

        ps = ctx.enter_context(nc.psum_tensor("ps", [P, 8, 512], F32))

        def bank_b(i):
            return ps[:, i, :].bitcast(BF16)

        x_loaded = [sem(f"x_loaded{i}") for i in range(NX)]
        weights_loaded = sem("weights_loaded")
        stats_done = sem("stats_done")
        dve_step = sem("dve_step")
        var_ready = sem("var_ready")
        std_ready = sem("std_ready")
        xn_ready = sem("xn_ready")
        xt_done = sem("xt_done")
        xt_out = sem("xt_out")
        qkv_done = sem("qkv_done")
        qkv_out = sem("qkv_out")
        rope_done = sem("rope_done")
        pt_done = sem("pt_done")
        pt_out = sem("pt_out")
        parts_stored = sem("parts_stored")
        hit_ready = sem("hit_ready")
        choice_ready = sem("choice_ready")
        g_done = sem("g_done")
        mask_done = sem("mask_done")
        u_done = sem("u_done")
        relu_done = sem("relu_done")
        masked = sem("masked")
        squared = sem("squared")
        inter_ready = sem("inter_ready")
        wd_done = sem("wd_done")
        ey_ready = sem("ey_ready")
        gate_ready = sem("gate_ready")
        consts_ready = sem("consts_ready")
        a_loaded = [sem(f"a_loaded{i}") for i in range(2)]
        a_scored = sem("a_scored")
        a_reduced = [sem(f"a_reduced{i}") for i in range(2)]
        mparts_ready = sem("mparts_ready")
        mt_done = sem("mt_done")
        mrow_ready = sem("mrow_ready")
        shift_stored = sem("shift_stored")
        loaded = [sem(f"loaded{i}") for i in range(2)]
        scored_half = [sem(f"scored_half{i}") for i in range(2)]
        exp_done = [sem(f"exp_done{i}") for i in range(2)]
        pv_done = [sem(f"pv_done{i}") for i in range(2)]
        v_staged = [sem(f"v_staged{i}") for i in range(2)]
        o_out = [sem(f"o_out{i}") for i in range(2)]
        o_stored = [sem(f"o_stored{i}") for i in range(2)]
        end_loaded = sem("end_loaded")
        normed = sem("normed")
        proj_done = sem("proj_done")
        res_ready = [sem(f"res_ready{i}") for i in range(2)]
        res_stored = [sem(f"res_stored{i}") for i in range(2)]

        NW = 8
        NP = NH // 2
        NB2 = KB // 2
        ENDT = KB // 2
        SETUP_STEPS = 8

        from_one = [rope_done, hit_ready, masked, parts_stored, squared, inter_ready, gate_ready, pt_done, qkv_out,
                    pt_out, wd_done, mask_done, *pv_done, *exp_done, *o_out, *o_stored, *a_reduced]

        counters_set = sem("counters_set")

        def past(n):
            return n + 1

        block = ctx.enter_context(nc.Block())

        def stack_loads(eng, b, h, s, done, shift_row=None):
            for qk, stack, order in ((0, qst, QPARTS), (1, kst, KPARTS)):
                for i in range(2):
                    dst = stack[s][3 * DH * i:3 * DH * (i + 1), :]
                    if qk == 0:
                        src = parts_d[order[3 * i], qk, bass.ds(h * DH, DH), bass.ds(b * L, L)]
                        src = src.unsqueeze(0).to_broadcast([3, DH, L])
                    else:
                        src = parts_d[:, qk, bass.ds(h * DH, DH), bass.ds(b * L, L)]
                    eng.dma_start(dst, src).then_inc(done, 16)
                src = parts_d[order[6], qk, bass.ds(h * DH, DH), bass.ds(b * L, L)]
                eng.dma_start(stack[s][6 * DH:7 * DH, :], src).then_inc(done, 16)
            if shift_row is not None:
                eng.dma_start(qst[s][KR:KS, :], shift_d[:, bass.ds(shift_row, L)]).then_inc(done, 16)

        @block.sync
        def _(sp):
            n = NT // NX
            for i in range(NX):
                sp.dma_start(x_sb[:, i * n:(i + 1) * n, :], x_v[:, i * n:(i + 1) * n, :]).then_inc(x_loaded[i], 16)

            sp.wait_ge(counters_set, 1)
            with sp.Fori(0, NG) as g:
                sp.wait_ge(pt_out, past(g * (2 * GT) + 2 * GT))
                sp.dma_start(parts_d.rearrange("a k (c p) t -> p (a k c) t", p=P)[:, :, bass.ds(g * W, W)],
                             pst).then_inc(parts_stored, 16)
            sp.wait_ge(parts_stored, past(16 * NG))
            sp.wait_ge(gate_ready, past(2 * NG))
            sp.wait_ge(consts_ready, 2)

            def a_pair(b, j, s, pi):
                stack_loads(sp, b, j * 2 + s, s, a_loaded[s])

            for s in range(2):
                a_pair(0, 0, s, 0)
            with sp.Fori(1, H // 2) as j:
                for s in range(2):
                    sp.wait_ge(a_scored, (j * 2 + s - 1) * KB)
                    a_pair(0, j, s, j)
            with sp.Fori(0, H // 2) as j:
                for s in range(2):
                    sp.wait_ge(a_scored, (j * 2 + s + H - 1) * KB)
                    a_pair(1, j, s, j)
            sp.wait_ge(mrow_ready, NPART)
            sp.dma_start(shift_d.rearrange("a (c r q) -> r a c q", r=P, q=P),
                         mrow.rearrange("p a (c q) -> p a c q", q=P)).then_inc(shift_stored, 16)
            sp.wait_ge(shift_stored, 16)

            def load(b, j, s, n):
                stack_loads(sp, b, j * 2 + s, s, loaded[s], shift_row=n * L)

            def store(b, j, s, pi):
                sp.wait_ge(o_out[s], past(pi + 1))
                h = j * 2 + s
                for c in range(QT):
                    sp.dma_start(onum_d[b, bass.ds(h * DH, DH), c * W:(c + 1) * W],
                                 osb[s][32 * c + 1:32 * c + 1 + DH, :]).then_inc(o_stored[s], 16)
                sp.dma_start(orec_d[b, bass.ds(h, 1), :].rearrange("d (c t) -> (d c) t", c=QT),
                             orc[s][0:P:32, :]).then_inc(o_stored[s], 16)

            for s in range(2):
                load(0, 0, s, s)
            with sp.Fori(1, H // 2) as j:
                for s in range(2):
                    sp.wait_ge(scored_half[1], j * (2 * KB) + (s - 1) * KB)
                    load(0, j, s, j * 2 + s)
                    store(0, j - 1, s, j - 1)
            for s in range(2):
                sp.wait_ge(scored_half[1], H * KB + (s - 1) * KB)
                load(1, 0, s, H + s)
                store(0, H // 2 - 1, s, H // 2 - 1)
            with sp.Fori(1, H // 2) as j:
                for s in range(2):
                    sp.wait_ge(scored_half[1], j * (2 * KB) + (H + s - 1) * KB)
                    load(1, j, s, j * 2 + s + H)
                    store(1, j - 1, s, j + (H // 2 - 1))
            for s in range(2):
                store(1, H // 2 - 1, s, NP - 1)
            for s in range(2):
                sp.wait_ge(o_stored[s], past(16 * STORES * NP))

            def end_load(b):
                for c in range(KC):
                    sp.dma_start(onum[:, c, :], onum_d[b, c * P:(c + 1) * P, :]).then_inc(end_loaded, 16)
                    src = orec_d[b, c * P // DH:(c + 1) * P // DH, :].unsqueeze(1).to_broadcast([P // DH, DH, L])
                    sp.dma_start(orec[:, c, :], src).then_inc(end_loaded, 16)

            end_load(0)
            sp.wait_ge(proj_done, ENDT)
            end_load(1)

        @block.scalar
        def _(act):
            for dst, src in ((ident, ident_in), (w_sb, w_in), (wg_sb, wg_in), (wu_sb, wu_in), (rope, rope_in),
                             (rank, rank_in), (wd_sb, wd_in), (wo_sb, wout_in)):
                act.dma_start(dst[:], src).then_inc(weights_loaded, 16)

            act.wait_ge(counters_set, 1)
            act.wait_ge(var_ready, 1)
            nc.scalar.activation(tmp[:, 3, :], tmp[:, 2, :], ACT.Sqrt).then_inc(std_ready, 1)

            def xt_copy(n, s):
                for i in range(2):
                    act.wait_ge(xt_done, n * 2 + (i + 1))
                    nc.scalar.copy(xnT[s][:, :, i * 2 * P:(i + 1) * 2 * P],
                                   ps[:, 6 + i, :].rearrange("p (k t) -> p k t", k=KC)).then_inc(xt_out, 1)

            def group(n, s, has_next):
                if True:
                    act.wait_ge(rope_done, past(n * GT))
                    act.wait_ge(hit_ready, past(n))
                for j in range(GT):
                    o = 2 * (j % 2)
                    act.wait_ge(qkv_done, n * GT + (j + 1))
                    nc.scalar.copy(qk_s[j], ps[:, o, :])
                    nc.scalar.activation(qk_q[j], ps[:, o, :], ACT.Square)
                    nc.scalar.copy(v_sb[:, bass.ds(n * GT + j, 1), :], ps[:, o + 1, 0:D].unsqueeze(1))
                    nc.scalar.copy(logit[:, j, :], ps[:, o + 1, D:VG]).then_inc(qkv_out, 1)
                if has_next:
                    xt_copy(n + 1, 1 - s)
                for c in range(EC):
                    act.wait_ge(g_done, n * EC + (c + 1))
                    act.wait_ge(masked, past(n * EC + max(c - 1, 0)))
                    nc.scalar.activation(hid[c % 2], ps[:, 2 * (c % 2), :], ACT.Relu).then_inc(relu_done, 1)
                    for i in range(2):
                        if c == 0 and i == 0:
                            act.wait_ge(parts_stored, past(n * 16))
                        act.wait_ge(pt_done, past((n * GT + c) * 2 + i + 1))
                        nc.scalar.copy(pst[:, i * HM:(i + 1) * HM, c * P:(c + 1) * P],
                                       bank_b(5)[:, 0:HM * P].rearrange("p (m t) -> p m t", m=HM)).then_inc(pt_out, 1)
                        if i == 0:
                            act.wait_ge(masked, past(n * EC + (c + 1)))
                            act.wait_ge(inter_ready, past(n * EC + max(c - 1, 0)))
                            nc.scalar.activation(hid_q[c % 2], hid_m[c % 2], ACT.Square).then_inc(squared, 1)
                for i in range(2):
                    act.wait_ge(gate_ready, past(n * 2))
                    act.wait_ge(wd_done, past(n * 2 + (i + 1)))
                    nc.scalar.activation(ey[i], ps[:, 6 + i, :].rearrange("p (t d) -> p t d", d=D), ACT.Exp,
                                         scale=-1.0).then_inc(ey_ready, 1)

            xt_copy(0, 0)
            with act.Fori(0, NG // 2 - 1) as gp:
                for s in range(2):
                    group(gp * 2 + s, s, True)
            group(NG - 2, 0, True)
            group(NG - 1, 1, False)

            with act.Fori(0, NP) as pi:
                for s in range(2):
                    for kb in range(KB):
                        g = pi * (2 * KB) + (s * KB + kb)
                        act.wait_ge(pv_done[kb % 2], past(pi * KB + (s * NB2 + kb // 2)))
                        for u in range(2):
                            act.wait_ge(scored_half[u], g + 1)
                            nc.scalar.activation(prob[kb % 2][:, 2 * u * W:2 * (u + 1) * W].rearrange(
                                "p (a t) -> p a t", a=2), ps[:, 2 * u:2 * u + 2, :], ACT.Exp,
                                scale=SCALE).then_inc(exp_done[u], 1)

            for b in range(B):
                for i in range(ENDT):
                    n = b * ENDT + i
                    act.wait_ge(res_ready[i % 2], n // 2 + 1)
                    act.dma_start(out_v[:, 2 * n:2 * n + 2, :], res[i % 2]).then_inc(res_stored[i % 2], 16)
            for i in range(2):
                act.wait_ge(res_stored[i], 16 * B * ENDT // 2)

        @block.vector
        def _(dve):
            base, count = [0], [0]

            def link(ins):
                count[0] += 1
                ins.then_inc(dve_step, 1)
                dve.wait_ge(dve_step, base[0] + count[0])

            def memset_ones():
                for s in range(2):
                    nc.vector.memset(vst[s], 1.0)
                    nc.vector.memset(kst[s][96:KS, :], 1.0).then_inc(consts_ready, 1)

            dve.wait_ge(counters_set, 1)
            for i in range(NX):
                dve.wait_ge(x_loaded[i], 16)
                with dve.Fori(0, NT // NX) as t:
                    nc.vector.bn_stats(stats[:, bass.ds(t + i * (NT // NX), 1), :],
                                       x_sb[:, bass.ds(t + i * (NT // NX), 1), :]).then_inc(stats_done, 1)
            dve.wait_ge(stats_done, NT)
            link(nc.vector.tensor_tensor(mean[:], stats[:, :, 1], stats[:, :, 4], ALU.add))
            link(nc.vector.tensor_scalar(mean[:], mean[:], 0.5, None, ALU.mult))
            link(nc.vector.tensor_tensor(tmp[:, 0, :], stats[:, :, 1], stats[:, :, 4], ALU.subtract))
            link(nc.vector.tensor_tensor(tmp[:, 0, :], tmp[:, 0, :], tmp[:, 0, :], ALU.mult))
            link(nc.vector.tensor_tensor(tmp[:, 1, :], stats[:, :, 2], stats[:, :, 5], ALU.add))
            link(nc.vector.tensor_scalar(tmp[:, 1, :], tmp[:, 1, :], 1.0 / D, EPS, ALU.mult, ALU.add))
            nc.vector.scalar_tensor_tensor(out=tmp[:, 2, :], in0=tmp[:, 0, :], scalar=0.25, in1=tmp[:, 1, :],
                                           op0=ALU.mult, op1=ALU.add).then_inc(var_ready, 1)
            dve.wait_ge(std_ready, 1)
            link(nc.vector.reciprocal(rstd[:], tmp[:, 3, :]))
            dve.wait_ge(weights_loaded, 16 * NW)
            link(nc.vector.tensor_copy(ident_b[:], ident[:]))

            def norm(n, s, first=False):
                if not first:
                    dve.wait_ge(xt_done, n * 2 - 2)
                for j in range(GT):
                    t = bass.ds(n * GT + j, 1)
                    ins = nc.vector.tensor_scalar(xn[s][:, j, :], x_sb[:, t, :], mean[:, t], rstd[:, t],
                                                  ALU.subtract, ALU.mult)
                ins.then_inc(xn_ready, 1)

            def rotate(n, j):
                t = n * GT + j
                tab = rope[:, bass.ds(t, 1), :]
                hd = DH // 2
                dve.wait_ge(qkv_out, past(t + 1))
                dve.wait_ge(rope_done, past(t))
                q2 = qk_s[j].rearrange("p (h d) -> p h d", d=hd)
                q4 = qk_s[j].rearrange("p (h a d) -> p h a d", a=2, d=hd)
                b4 = rb.rearrange("p (h a d) -> p h a d", a=2, d=hd)
                nc.vector.tensor_tensor(ra.rearrange("p (h d) -> p h d", d=hd), q2,
                                        tab[:, :, 0:hd].to_broadcast([P, 2 * QK // DH, hd]), ALU.mult)
                nc.vector.tensor_tensor(b4[:, :, 0, :], q4[:, :, 1, :],
                                        tab[:, :, 2 * hd:3 * hd].to_broadcast([P, QK // DH, hd]), ALU.mult)
                link(nc.vector.tensor_tensor(b4[:, :, 1, :], q4[:, :, 0, :],
                                             tab[:, :, hd:2 * hd].to_broadcast([P, QK // DH, hd]), ALU.mult))
                link(nc.vector.tensor_tensor(rq, ra, rb, ALU.add))
                if j < 2:
                    dve.wait_ge(pt_done, past(n * (2 * GT)))
                else:
                    dve.wait_ge(pt_done, past(t * 2 - 2))
                part = parts[j % 2]
                link(nc.vector.tensor_copy(part[:, 0, :], rq))
                link(nc.vector.tensor_tensor(ra, rq, part[:, 0, :], ALU.subtract))
                link(nc.vector.tensor_copy(part[:, 1, :], ra))
                nc.vector.tensor_tensor(part[:, 2, :], ra, part[:, 1, :], ALU.subtract).then_inc(rope_done, 1)

            def route(n):
                dve.wait_ge(qkv_out, past(n * GT + GT))
                dve.wait_ge(hit_ready, past(n))
                full = [P, GT, E]
                link(nc.vector.tensor_reduce(best, logit, AX.X, ALU.max))
                link(nc.vector.tensor_tensor(hit, logit, best.unsqueeze(2).to_broadcast(full), ALU.is_equal))
                link(nc.vector.tensor_tensor(hit, hit, rank[:].unsqueeze(1).to_broadcast(full), ALU.mult))
                link(nc.vector.tensor_reduce(best, hit, AX.X, ALU.max))
                dve.wait_ge(choice_ready, n)
                nc.vector.tensor_tensor(won, hit, best.unsqueeze(2).to_broadcast(full),
                                        ALU.is_equal).then_inc(hit_ready, 1)

            def expert(n, c):
                m = n * EC + c
                dve.wait_ge(relu_done, m + 1)
                dve.wait_ge(mask_done, past(m + 1))
                dve.wait_ge(squared, past(n * EC + max(c - 1, 0)))
                nc.vector.tensor_tensor(hid_m[c % 2], hid[c % 2], ps[:, 4, :], ALU.mult).then_inc(masked, 1)
                dve.wait_ge(squared, past(m + 1))
                dve.wait_ge(u_done, m + 1)
                if c == 0:
                    dve.wait_ge(wd_done, past(n * 2))
                nc.vector.tensor_tensor(inter[:, c, :], hid_q[c % 2], ps[:, 1 + 2 * (c % 2), :],
                                        ALU.mult).then_inc(inter_ready, 1)

            def silu(n):
                for i in range(2):
                    dve.wait_ge(ey_ready, n * 2 + (i + 1))
                    link(nc.vector.tensor_scalar(ey[i], ey[i], 1.0, None, ALU.add))
                    link(nc.vector.reciprocal(ey[i], ey[i]))
                    nc.vector.tensor_tensor(gate[:, bass.ds(n * GT + 2 * i, 2), :],
                                            ps[:, 6 + i, :].rearrange("p (t d) -> p t d", d=D), ey[i],
                                            ALU.mult).then_inc(gate_ready, 1)

            STEPS = 4 * 5 + 4 + 4

            def group(n, s, has_next):
                rotate(n, 0)
                if has_next:
                    norm(n + 1, 1 - s)
                rotate(n, 1)
                route(n)
                expert(n, 0)
                rotate(n, 2)
                expert(n, 1)
                rotate(n, 3)
                expert(n, 2)
                expert(n, 3)
                silu(n)

            assert count[0] == SETUP_STEPS
            norm(0, 0, first=True)
            with dve.Fori(0, NG // 2 - 1) as gp:
                base[0], count[0] = gp * (2 * STEPS) + SETUP_STEPS, 0
                for s in range(2):
                    group(gp * 2 + s, s, True)
                assert count[0] == 2 * STEPS
            base[0], count[0] = SETUP_STEPS + (NG - 2) * STEPS, 0
            group(NG - 2, 0, True)
            group(NG - 1, 1, False)

            dve.wait_ge(parts_stored, past(16 * NG))
            memset_ones()

            with dve.Fori(0, NP) as pi:
                for s in range(2):
                    for t in range(KB):
                        m = pi * (2 * KB) + (s * KB + t)
                        dve.wait_ge(a_scored, m + 1)
                        o = 4 * (t % 2)
                        nc.vector.tensor_reduce(negm[:, bass.ds(m, 1)], ps[:, o:o + 4, :], AX.XY, ALU.max,
                                                negate=True).then_inc(a_reduced[t % 2], 1)
            for i in range(2):
                dve.wait_ge(a_reduced[i], past(NH * NB2))
            link(nc.vector.tensor_copy(mpart[:, 0, :], negm[:]))
            link(nc.vector.tensor_tensor(mres, negm[:], mpart[:, 0, :], ALU.subtract))
            link(nc.vector.tensor_copy(mpart[:, 1, :], mres))
            nc.vector.tensor_tensor(mpart[:, 2, :], mres, mpart[:, 1, :], ALU.subtract).then_inc(mparts_ready, 1)
            for a in range(NPART):
                dve.wait_ge(mt_done, a + 1)
                nc.vector.tensor_copy(mrow[:, a, :], bank_b(a)[:, 0:NH * KB]).then_inc(mrow_ready, 1)

            with dve.Fori(0, NP) as pi:
                for s in range(2):
                    dve.wait_ge(pv_done[1], past(pi * KB + (s + 1) * NB2))
                    dve.wait_ge(o_stored[s], past(pi * (16 * STORES)))
                    nc.vector.tensor_copy(osb[s], ps[:, 4 + s, :])
                    for c in range(QT):
                        ins = nc.vector.reciprocal(orc[s][32 * c:32 * c + 1, :], ps[32 * c:32 * c + 1, 4 + s, :])
                    ins.then_inc(o_out[s], 1)

            base[0], count[0] = base[0] + count[0], 0
            for b in range(B):
                dve.wait_ge(end_loaded, 16 * 2 * KC * (b + 1))
                for i in range(2 * QT):
                    c, t = i % KC, i // KC
                    sl = onum[:, c, t * W:(t + 1) * W]
                    nc.vector.tensor_tensor(sl, sl, orec[:, c, t * W:(t + 1) * W], ALU.mult).then_inc(normed, 1)
                for i in range(ENDT):
                    n = b * ENDT + i
                    dve.wait_ge(proj_done, n + 1)
                    if n >= 2:
                        dve.wait_ge(res_stored[i % 2], 16 * (n // 2))
                    link(nc.vector.tensor_tensor(res[i % 2], ps[:, i % 4, :].rearrange("p (t d) -> p t d", d=D),
                                                 gate[:, 2 * n:2 * n + 2, :], ALU.mult))
                    nc.vector.tensor_tensor(res[i % 2], res[i % 2], x_sb[:, 2 * n:2 * n + 2, :],
                                            ALU.add).then_inc(res_ready[i % 2], 1)

        @block.gpsimd
        def _(pool):
            for counter in from_one:
                pool.sem_inc(counter, 1)
            pool.sem_inc(counters_set, 1)
            with pool.Fori(0, NG) as n:
                pool.wait_ge(hit_ready, past(n + 1))
                pool.wait_ge(mask_done, past(n * EC))
                many = won.unsqueeze(3).to_broadcast([P, GT, E, DE])
                nc.gpsimd.tensor_tensor(choice, many, many, ALU.mult).then_inc(choice_ready, 1)

            def stage(b, j, s, pi):
                pool.wait_ge(o_out[s], past(pi))
                h = j * 2 + s
                pool.wait_ge(consts_ready, 2)
                nc.gpsimd.tensor_copy(vst[s][:, :, 1:1 + DH],
                                      v_sb[:, b * KB:(b + 1) * KB, bass.ds(h * DH, DH)]).then_inc(v_staged[s], 1)

            pool.wait_ge(consts_ready, 2)
            for b in range(B):
                with pool.Fori(0, H // 2) as j:
                    for s in range(2):
                        stage(b, j, s, j + b * (H // 2))

        @block.tensor
        def _(pe):
            pe.wait_ge(counters_set, 1)
            pe.wait_ge(weights_loaded, 16 * NW)
            pe.wait_ge(dve_step, SETUP_STEPS)

            def transpose_x(n, s):
                pe.wait_ge(xn_ready, n + 1)
                for j in range(GT):
                    for k in range(KC):
                        last = nc.tensor.transpose(ps[:, 6 + j // 2, (2 * k + j % 2) * P:(2 * k + j % 2 + 1) * P],
                                                   xn[s][:, j, k * P:(k + 1) * P], ident[:])
                    if j % 2:
                        last.then_inc(xt_done, 1)

            def group(n, s, has_next):
                pe.wait_ge(xt_out, n * 2 + 2)
                for j in range(GT):
                    o = 2 * (j % 2)
                    if j < 2:
                        pe.wait_ge(inter_ready, past(n * EC))
                    else:
                        pe.wait_ge(qkv_out, past(n * GT + j - 1))
                    for k in range(KC):
                        xt = xnT[s][:, k, j * P:(j + 1) * P]
                        nc.tensor.matmul(ps[:, o, :], xt, w_sb[:, k, 0:QK], start=(k == 0), stop=(k == KC - 1))
                        last = nc.tensor.matmul(ps[:, o + 1, 0:VG], xt, w_sb[:, k, QK:QK + VG],
                                                start=(k == 0), stop=(k == KC - 1))
                    last.then_inc(qkv_done, 1)
                pe.wait_ge(gate_ready, past(n * 2))
                if has_next:
                    transpose_x(n + 1, 1 - s)
                for c in range(EC):
                    m = n * EC + c
                    o = 2 * (c % 2)
                    if c < 2:
                        pe.wait_ge(qkv_out, past(n * GT + (c + 3)))
                    else:
                        pe.wait_ge(inter_ready, past(m - 1))
                    for k in range(KC):
                        last = nc.tensor.matmul(ps[:, o, :], wg_sb[:, k, c * P:(c + 1) * P], xnT[s][:, k, :],
                                                start=(k == 0), stop=(k == KC - 1))
                    last.then_inc(g_done, 1)
                    if c == 0:
                        pe.wait_ge(choice_ready, n + 1)
                    pe.wait_ge(masked, past(m))
                    for j in range(GT):
                        last = nc.tensor.matmul(ps[:, 4, j * P:(j + 1) * P],
                                                choice[:, j, :, :].rearrange("p e d -> p (e d)")[:, c * P:(c + 1) * P],
                                                ident_b[:], start=True, stop=True)
                    last.then_inc(mask_done, 1)
                    for i in range(2):
                        if i == 0:
                            pe.wait_ge(rope_done, past(m + 1))
                        else:
                            for k in range(KC):
                                last = nc.tensor.matmul(ps[:, o + 1, :], wu_sb[:, k, c * P:(c + 1) * P],
                                                        xnT[s][:, k, :], start=(k == 0), stop=(k == KC - 1))
                            last.then_inc(u_done, 1)
                        pe.wait_ge(pt_out, past(m * 2 + i))
                        for q in range(HM):
                            a, kc = divmod(i * HM + q, 2 * KC)
                            last = nc.tensor.transpose(bank_b(5)[:, q * P:(q + 1) * P],
                                                       parts[c % 2][:, a, kc * P:(kc + 1) * P], ident_b[:])
                        last.then_inc(pt_done, 1)
                pe.wait_ge(inter_ready, past(n * EC + EC))
                if has_next:
                    pe.wait_ge(xt_out, n * 2 + 4)
                for j in range(GT):
                    for c in range(EC):
                        last = nc.tensor.matmul(ps[:, 6 + j // 2, (j % 2) * D:(j % 2 + 1) * D],
                                                inter[:, c, j * P:(j + 1) * P], wd_sb[:, c, :],
                                                start=(c == 0), stop=(c == EC - 1))
                    if j % 2:
                        last.then_inc(wd_done, 1)

            transpose_x(0, 0)
            with pe.Fori(0, NG // 2 - 1) as gp:
                for s in range(2):
                    group(gp * 2 + s, s, True)
            group(NG - 2, 0, True)
            group(NG - 1, 1, False)

            pe.wait_ge(pt_out, past(2 * NT))
            pe.wait_ge(gate_ready, past(2 * NG))
            with pe.Fori(0, NP) as pi:
                for s in range(2):
                    pe.wait_ge(a_loaded[s], pi * (16 * (LOADS - 1)) + 16 * (LOADS - 1))
                    for t in range(KB):
                        pe.wait_ge(a_reduced[t % 2], past(pi * KB + (s * NB2 + t // 2)))
                        for c in range(QT):
                            last = nc.tensor.matmul(ps[:, 4 * (t % 2) + c, :], qst[s][0:KR, t * P:(t + 1) * P],
                                                    kst[s][0:KR, c * W:(c + 1) * W], start=True, stop=True)
                        last.then_inc(a_scored, 1)
            pe.wait_ge(mparts_ready, 1)
            for a in range(NPART):
                for c in range(NH * KB // P):
                    last = nc.tensor.transpose(bank_b(a)[:, c * P:(c + 1) * P], mpart[:, a, c * P:(c + 1) * P],
                                               ident_b[:])
                last.then_inc(mt_done, 1)
            pe.wait_ge(mrow_ready, NPART)

            def score(s, kb, g):
                for u in range(2):
                    pe.wait_ge(exp_done[u], past(g))
                    for c in (2 * u, 2 * u + 1):
                        last = nc.tensor.matmul(ps[:, c, :], kst[s][0:KS, kb * P:(kb + 1) * P],
                                                qst[s][0:KS, c * W:(c + 1) * W], start=True, stop=True)
                    last.then_inc(scored_half[u], 1)

            def pair(pi, last_pair):
                for s in range(2):
                    for kb in range(KB):
                        g = pi * (2 * KB) + (s * KB + kb)
                        if kb < KB - 1:
                            score(s, kb + 1, g + 1)
                        elif s == 0:
                            pe.wait_ge(loaded[1], (pi + 1) * (16 * LOADS))
                            score(1, 0, g + 1)
                        elif not last_pair:
                            pe.wait_ge(loaded[0], (pi + 2) * (16 * LOADS))
                            score(0, 0, g + 1)
                        if kb == 0:
                            pe.wait_ge(v_staged[s], pi + 1)
                            pe.wait_ge(o_out[s], past(pi))
                        for c in range(QT):
                            if c % 2 == 0:
                                pe.wait_ge(exp_done[c // 2], past(g + 1))
                            last = nc.tensor.matmul(ps[32 * c:32 * (c + 1), 4 + s, :], vst[s][:, kb, :],
                                                    prob[kb % 2][:, c * W:(c + 1) * W],
                                                    start=(kb == 0), stop=(kb == KB - 1))
                        last.then_inc(pv_done[kb % 2], 1)

            pe.wait_ge(loaded[0], 16 * LOADS)
            score(0, 0, 0)
            with pe.Fori(0, NP - 1) as pi:
                pair(pi, False)
            pair(NP - 1, True)

            for b in range(B):
                for i in range(ENDT):
                    n = b * ENDT + i
                    pe.wait_ge(normed, b * 2 * QT + KC * (i // 2 + 1))
                    if n >= 4:
                        pe.wait_ge(res_ready[i % 2], n // 2 - 1)
                    for t in range(2):
                        for k in range(KC):
                            last = nc.tensor.matmul(ps[:, i % 4, t * D:(t + 1) * D],
                                                    onum[:, k, (2 * i + t) * P:(2 * i + t + 1) * P], wo_sb[:, k, :],
                                                    start=(k == 0), stop=(k == KC - 1))
                    last.then_inc(proj_done, 1)


def kernel(L0_attn_x, L0_attn_w_qkv, L0_attn_w_out, L0_ffn_gate_w, L0_ffn_wg, L0_ffn_wu, L0_ffn_wd):
    import numpy as np
    import concourse.bacc as bacc
    from concourse import mybir
    from concourse.bass_utils import run_bass_kernel_spmd

    def rows(a):
        return np.ascontiguousarray(a.reshape(-1, 128, a.shape[-1]).transpose(1, 0, 2))

    x = np.ascontiguousarray(L0_attn_x)
    e, d, f = L0_ffn_wg.shape
    length, half = x.shape[1], 8
    inv = np.float32(1.0) / np.float32(10000.0) ** (np.arange(half, dtype=np.float32) / np.float32(half))
    ang = np.arange(length, dtype=np.float32)[:, None] * inv[None, :].astype(np.float32)
    table = np.concatenate([np.cos(ang), np.sin(ang), -np.sin(ang)], axis=-1).astype(np.float32)
    arrays = {
        "x": x,
        "w": rows(np.concatenate([np.asarray(L0_attn_w_qkv), np.asarray(L0_ffn_gate_w)], axis=0).T),
        "wout": rows(np.asarray(L0_attn_w_out).T),
        "wg": rows(np.asarray(L0_ffn_wg).transpose(1, 0, 2).reshape(d, e * f)),
        "wu": rows(np.asarray(L0_ffn_wu).transpose(1, 0, 2).reshape(d, e * f)),
        "wd": rows(np.asarray(L0_ffn_wd).reshape(e * f, d)),
        "rope": np.tile(rows(table), (1, x.shape[0], 1)),
        "ident": np.eye(128, dtype=np.float32),
        "rank": np.tile(np.arange(e, 0, -1, dtype=np.float32), (128, 1)),
    }
    nc = bacc.Bacc("TRN2", target_bir_lowering=False, num_devices=1)
    args, feed = [], {}
    for name, a in arrays.items():
        feed[f"in_{name}"] = a
        args.append(nc.dram_tensor(f"in_{name}", a.shape, mybir.dt.from_np(a.dtype), kind="ExternalInput").ap())
    args.append(nc.dram_tensor("out", x.shape, mybir.dt.float32, kind="ExternalOutput").ap())
    layer_kernel(nc, *args)
    got = run_bass_kernel_spmd(nc, [feed], core_ids=[0])
    return got.results[0]["out"]
```

```python
import concourse.bass as bass
from concourse import mybir
from contextlib import ExitStack


def layer_kernel(nc, x_in, w_in, wout_in, wg_in, wu_in, wd_in, rope_in, ident_in, rank_in, out):
    F32, BF16 = mybir.dt.float32, mybir.dt.bfloat16
    ALU, ACT, AX = mybir.AluOpType, mybir.ActivationFunctionType, mybir.AxisListType

    B, L, D = 2, 2048, 256
    H, DH = 16, 16
    E, DE = 8, 64
    P = 128
    NT = B * L // P
    GT = 4
    NG = NT // GT
    W = GT * P
    KC = D // P
    NX = 4
    EC = E * DE // P
    QK = 2 * D
    VG = D + E
    NPART = 3
    QPARTS = (0, 0, 0, 1, 1, 1, 2)
    KPARTS = (0, 1, 2, 0, 1, 2, 0)
    KR = DH * len(QPARTS)
    KS = KR + NPART
    NM = NPART * 2 * KC
    HM = NM // 2
    NH = B * H
    KB = L // P
    QT = L // W
    SCALE = DH ** -0.5
    EPS = 1e-5
    NC = B * KC
    CP = NH // 2 // NC
    LOADS = 6
    AHEAD = KB + 3

    x_v = x_in.rearrange("b (t p) d -> p (b t) d", p=P)
    out_v = out.rearrange("b (t p) d -> p (b t) d", p=P)

    ctx = ExitStack()
    with ctx:
        def sb(name, shape, dt=F32):
            return ctx.enter_context(nc.sbuf_tensor(name, shape, dt))

        def sem(name):
            return ctx.enter_context(nc.semaphore(name))

        parts_d = nc.dram_tensor("parts_d", (NPART, 2, B * D, L), BF16, kind="Internal").ap()
        onum_d = nc.dram_tensor("onum_d", (B * D, L), F32, kind="Internal").ap()
        orec_d = nc.dram_tensor("orec_d", (NH, L), F32, kind="Internal").ap()

        x_sb = sb("x_sb", [P, NT, D])
        v_sb = sb("v_sb", [P, NT, D])
        gate = sb("gate", [P, NT, D])
        wo_sb = sb("wo_sb", [P, KC, D])
        rope = sb("rope", [P, NT, 3 * DH // 2])
        ident = sb("ident", [P, P])
        ident_b = sb("ident_b", [P, P], BF16)
        rank = sb("rank", [P, E])
        stats = sb("stats", [P, NT, 6])
        mean = sb("mean", [P, NT])
        rstd = sb("rstd", [P, NT])
        tmp = sb("tmp", [P, 4, NT])

        ARENA = 25104
        arena = sb("arena", [P, ARENA])
        at = [0]

        def cut(shape, dt=F32):
            n = 1
            for s in shape:
                n *= s
            words = n * (2 if dt == BF16 else 4) // 4
            flat = arena[:, at[0]:at[0] + words]
            at[0] += words
            assert at[0] <= ARENA
            if dt == BF16:
                flat = flat.bitcast(BF16)
            if len(shape) == 1:
                return flat
            names = "abcd"[:len(shape)]
            return flat.rearrange(f"p ({' '.join(names)}) -> p {' '.join(names)}", **dict(zip(names, shape)))

        w_sb = cut([KC, QK + VG])
        wg_sb = cut([KC, E * DE])
        wu_sb = cut([KC, E * DE])
        wd_sb = cut([EC, D])
        xn = [cut([GT, D]) for _ in range(2)]
        xnT = [cut([KC, W]) for _ in range(2)]
        qk_s = [cut([QK]) for _ in range(GT)]
        ra, rb, rq = cut([QK]), cut([QK]), cut([QK])
        parts = [cut([NPART, QK], BF16) for _ in range(2)]
        pst = cut([NM, W], BF16)
        hid = [cut([W]) for _ in range(2)]
        hid_m = [cut([W]) for _ in range(2)]
        hid_q = [cut([W]) for _ in range(2)]
        inter = cut([EC, W])
        choice = cut([GT, E, DE], BF16)
        logit = cut([GT, E])
        hit = cut([GT, E])
        won = cut([GT, E])
        best = cut([GT])
        assert at[0] <= ARENA
        at[0] = 0
        qa = [cut([L], BF16) for _ in range(2)]
        ka = [cut([L], BF16) for _ in range(2)]
        qst = [cut([L], BF16) for _ in range(2)]
        kst = [cut([L], BF16) for _ in range(2)]
        prob = [cut([L]) for _ in range(2)]
        vst = [cut([KB, 32]) for _ in range(2)]
        osb = [cut([W]) for _ in range(2)]
        most = [cut([KB, 2]) for _ in range(2)]
        negm = cut([KB])
        mres = cut([KB])
        mpart = cut([P], BF16)
        mrow = cut([P], BF16)
        spread = [cut([L // P]) for _ in range(2)]
        onum = cut([NC, L])
        orec = cut([L])
        assert at[0] <= ARENA
        at[0] = 0
        res = [cut([2, D]) for _ in range(2)]

        ps = ctx.enter_context(nc.psum_tensor("ps", [P, 8, 512], F32))

        def bank_b(i):
            return ps[:, i, :].bitcast(BF16)

        x_loaded = [sem(f"x_loaded{i}") for i in range(NX)]
        weights_loaded = sem("weights_loaded")
        stats_done = sem("stats_done")
        dve_step = sem("dve_step")
        var_ready = sem("var_ready")
        std_ready = sem("std_ready")
        xn_ready = sem("xn_ready")
        xt_done = sem("xt_done")
        xt_out = sem("xt_out")
        qkv_done = sem("qkv_done")
        qkv_out = sem("qkv_out")
        rope_done = sem("rope_done")
        pt_done = sem("pt_done")
        pt_out = sem("pt_out")
        parts_stored = sem("parts_stored")
        hit_ready = sem("hit_ready")
        choice_ready = sem("choice_ready")
        g_done = sem("g_done")
        mask_done = sem("mask_done")
        u_done = sem("u_done")
        relu_done = sem("relu_done")
        masked = sem("masked")
        squared = sem("squared")
        inter_ready = sem("inter_ready")
        wd_done = sem("wd_done")
        gate_ready = sem("gate_ready")
        consts_ready = sem("consts_ready")
        a_loaded = [sem(f"a_loaded{i}") for i in range(2)]
        a_scored = [sem(f"a_scored{i}") for i in range(2)]
        a_reduced = [sem(f"a_reduced{i}") for i in range(2)]
        mpart_ready = sem("mpart_ready")
        mt_done = sem("mt_done")
        mrow_ready = sem("mrow_ready")
        shift_loaded = [sem(f"shift_loaded{i}") for i in range(2)]
        loaded = [sem(f"loaded{i}") for i in range(2)]
        scored = [sem(f"scored{i}") for i in range(2)]
        exp_done = [sem(f"exp_done{i}") for i in range(2)]
        pv_done = [sem(f"pv_done{i}") for i in range(2)]
        v_staged = [sem(f"v_staged{i}") for i in range(2)]
        o_out = [sem(f"o_out{i}") for i in range(2)]
        o_stored = [sem(f"o_stored{i}") for i in range(2)]
        spread_in = [sem(f"spread_in{i}") for i in range(2)]
        rec_ready = [sem(f"rec_ready{i}") for i in range(2)]
        rec_stored = [sem(f"rec_stored{i}") for i in range(2)]
        chunk_loaded = sem("chunk_loaded")
        chunk_weighed = sem("chunk_weighed")
        normed = sem("normed")
        proj_done = sem("proj_done")
        res_ready = [sem(f"res_ready{i}") for i in range(2)]
        res_stored = [sem(f"res_stored{i}") for i in range(2)]

        PSTORES = 16 * NPART * 2
        NW = 8
        NP = NH // 2
        NB2 = KB // 2
        ENDT = KB // 2
        SETUP_STEPS = 8

        from_one = [rope_done, hit_ready, masked, parts_stored, squared, inter_ready, gate_ready, pt_done, qkv_out,
                    pt_out, wd_done, mask_done, *pv_done, *exp_done, *o_out, *o_stored, *a_reduced,
                    *spread_in, *rec_stored]

        counters_set = sem("counters_set")

        def past(n):
            return n + 1

        block = ctx.enter_context(nc.Block())

        def stack_loads(eng, head, qstack, kstack, done):
            rows = bass.ds(head * DH, DH)
            for qk, stack, order in ((0, qstack, QPARTS), (1, kstack, KPARTS)):
                for i in range(2):
                    if qk == 0:
                        src = parts_d[order[3 * i], qk, rows, :].unsqueeze(0).to_broadcast([3, DH, L])
                    else:
                        src = parts_d[:, qk, rows, :]
                    eng.dma_start(stack[3 * DH * i:3 * DH * (i + 1), :], src).then_inc(done, 16)
                eng.dma_start(stack[6 * DH:7 * DH, :], parts_d[order[6], qk, rows, :]).then_inc(done, 16)

        @block.sync
        def _(sp):
            n = NT // NX
            for i in range(NX):
                sp.dma_start(x_sb[:, i * n:(i + 1) * n, :], x_v[:, i * n:(i + 1) * n, :]).then_inc(x_loaded[i], 16)

            sp.wait_ge(counters_set, 1)
            for b in range(B):
                with sp.Fori(0, QT) as t:
                    sp.wait_ge(pt_out, past(t * (2 * GT) + (b * QT + 1) * 2 * GT))
                    for m in range(NPART * 2):
                        a, qk = divmod(m, 2)
                        sp.dma_start(parts_d[a, qk, b * D:(b + 1) * D, bass.ds(t * W, W)].rearrange(
                            "(c p) t -> p c t", p=P), pst[:, m * KC:(m + 1) * KC, :]).then_inc(parts_stored, 16)
            sp.wait_ge(parts_stored, past(PSTORES * NG))
            sp.wait_ge(gate_ready, past(2 * NG))
            sp.wait_ge(consts_ready, 2)

            def load_a(head, s):
                stack_loads(sp, head, qa[s], ka[s], a_loaded[s])

            def load(head, s):
                stack_loads(sp, head, qst[s], kst[s], loaded[s])

            def shift(head, s):
                sp.wait_ge(mrow_ready, head + 1)
                sp.dma_start(qst[s][KR:KS, :], mrow[0:NPART * KB, :]).then_inc(shift_loaded[s], 16)

            def store(head, s, pi):
                sp.wait_ge(o_out[s], past(pi + 1))
                sp.wait_ge(rec_stored[s], past(pi * 16))
                sp.dma_start(spread[s], osb[s][0:P:32, :]).then_inc(spread_in[s], 16)
                for c in range(QT):
                    sp.dma_start(onum_d[bass.ds(head * DH, DH), c * W:(c + 1) * W],
                                 osb[s][32 * c + 1:32 * c + 1 + DH, :]).then_inc(o_stored[s], 16)
                sp.wait_ge(rec_ready[s], pi + 1 + s)
                sp.dma_start(orec_d[bass.ds(head, 1), :].rearrange("h (c t) -> (h c) t", t=L // P),
                             spread[s]).then_inc(rec_stored[s], 16)

            def load_chunk(m):
                if m:
                    sp.wait_ge(chunk_weighed, m)
                for s in range(2):
                    sp.wait_ge(o_stored[s], past(16 * QT * CP * (m + 1)))
                sp.dma_start(onum[:, m, :], onum_d[m * P:(m + 1) * P, :]).then_inc(chunk_loaded, 16)
                for s in range(2):
                    sp.wait_ge(rec_stored[s], past(16 * CP * (m + 1)))
                src = orec_d[m * P // DH:(m + 1) * P // DH, :].unsqueeze(1).to_broadcast([P // DH, DH, L])
                sp.dma_start(orec, src).then_inc(chunk_loaded, 16)

            for s in range(2):
                load_a(s, s)
            for s in range(2):
                load(s, s)
            sp.wait_ge(a_scored[1], KB)
            load_a(2, 0)
            shift(0, 0)

            def pair(pi):
                for s in range(2):
                    n = pi * 2 + s
                    known = isinstance(n, int)
                    if not known or n + 3 < NH:
                        sp.wait_ge(a_scored[1], n * KB + 2 * KB)
                        load_a(n + 3, 1 - s)
                    if not known or n + 1 < NH:
                        shift(n + 1, 1 - s)
                    if not known or n + 2 < NH:
                        sp.wait_ge(scored[1], n * (2 * KB) + 2 * KB)
                        load(n + 2, s)
                    store(n, s, pi)

            for m in range(NC):
                peeled = 2 * (m == NC - 1)
                with sp.Fori(m * CP, (m + 1) * CP - peeled) as pi:
                    pair(pi)
                for pi in range((m + 1) * CP - peeled, (m + 1) * CP):
                    pair(pi)
                load_chunk(m)

        @block.scalar
        def _(act):
            for dst, src in ((ident[:], ident_in), (w_sb, w_in), (wg_sb, wg_in), (wu_sb, wu_in), (rope[:], rope_in),
                             (rank[:], rank_in), (wd_sb, wd_in), (wo_sb[:], wout_in)):
                act.dma_start(dst, src).then_inc(weights_loaded, 16)

            act.wait_ge(counters_set, 1)
            act.wait_ge(var_ready, 1)
            nc.scalar.activation(tmp[:, 3, :], tmp[:, 2, :], ACT.Sqrt).then_inc(std_ready, 1)

            def xt_copy(n, s):
                for i in range(2):
                    act.wait_ge(xt_done, n * 2 + (i + 1))
                    nc.scalar.copy(xnT[s][:, :, i * 2 * P:(i + 1) * 2 * P],
                                   ps[:, 6 + i, :].rearrange("p (k t) -> p k t", k=KC)).then_inc(xt_out, 1)

            def group(n, s, has_next):
                if True:
                    act.wait_ge(rope_done, past(n * GT))
                    act.wait_ge(hit_ready, past(n))
                for j in range(GT):
                    o = 2 * (j % 2)
                    act.wait_ge(qkv_done, n * GT + (j + 1))
                    nc.scalar.copy(qk_s[j], ps[:, o, :])
                    nc.scalar.copy(v_sb[:, bass.ds(n * GT + j, 1), :], ps[:, o + 1, 0:D].unsqueeze(1))
                    nc.scalar.copy(logit[:, j, :], ps[:, o + 1, D:VG]).then_inc(qkv_out, 1)
                if has_next:
                    xt_copy(n + 1, 1 - s)
                for c in range(EC):
                    act.wait_ge(g_done, n * EC + (c + 1))
                    act.wait_ge(masked, past(n * EC + max(c - 1, 0)))
                    nc.scalar.activation(hid[c % 2], ps[:, 2 * (c % 2), :], ACT.Relu).then_inc(relu_done, 1)
                    for i in range(2):
                        if c == 0 and i == 0:
                            act.wait_ge(parts_stored, past(n * PSTORES))
                        act.wait_ge(pt_done, past((n * GT + c) * 2 + i + 1))
                        nc.scalar.copy(pst[:, i * HM:(i + 1) * HM, c * P:(c + 1) * P],
                                       bank_b(5)[:, 0:HM * P].rearrange("p (m t) -> p m t", m=HM)).then_inc(pt_out, 1)
                        if i == 0:
                            act.wait_ge(masked, past(n * EC + (c + 1)))
                            act.wait_ge(inter_ready, past(n * EC + max(c - 1, 0)))
                            nc.scalar.activation(hid_q[c % 2], hid_m[c % 2], ACT.Square).then_inc(squared, 1)
                for i in range(2):
                    act.wait_ge(wd_done, past(n * 2 + (i + 1)))
                    nc.scalar.activation(gate[:, bass.ds(n * GT + 2 * i, 2), :],
                                         ps[:, 6 + i, :].rearrange("p (t d) -> p t d", d=D),
                                         ACT.Silu).then_inc(gate_ready, 1)

            xt_copy(0, 0)
            with act.Fori(0, NG // 2 - 1) as gp:
                for s in range(2):
                    group(gp * 2 + s, s, True)
            group(NG - 2, 0, True)
            group(NG - 1, 1, False)

            with act.Fori(0, NP) as pi:
                for s in range(2):
                    for kb in range(KB):
                        act.wait_ge(pv_done[kb % 2], past(pi * KB + (s * NB2 + kb // 2)))
                        for c in range(QT):
                            act.wait_ge(scored[c % 2], pi * (4 * KB) + (s * 2 * KB + kb * 2 + c // 2 + 1))
                            nc.scalar.activation(prob[kb % 2][:, c * W:(c + 1) * W], ps[:, c % 2, :], ACT.Exp,
                                                 scale=SCALE).then_inc(exp_done[c % 2], 1)

            for b in range(B):
                for i in range(ENDT):
                    n = b * ENDT + i
                    act.wait_ge(res_ready[i % 2], n // 2 + 1)
                    act.dma_start(out_v[:, 2 * n:2 * n + 2, :], res[i % 2]).then_inc(res_stored[i % 2], 16)
            for i in range(2):
                act.wait_ge(res_stored[i], 16 * B * ENDT // 2)

        @block.vector
        def _(dve):
            base, count = [0], [0]

            def link(ins):
                count[0] += 1
                ins.then_inc(dve_step, 1)
                dve.wait_ge(dve_step, base[0] + count[0])

            def memset_ones():
                nc.vector.memset(mpart, 0.0)
                nc.vector.memset(spread[1], 1.0)
                for s in range(2):
                    nc.vector.memset(vst[s], 1.0)
                    nc.vector.memset(kst[s][96:KS, :], 1.0).then_inc(consts_ready, 1)

            dve.wait_ge(counters_set, 1)
            for i in range(NX):
                dve.wait_ge(x_loaded[i], 16)
                with dve.Fori(0, NT // NX) as t:
                    nc.vector.bn_stats(stats[:, bass.ds(t + i * (NT // NX), 1), :],
                                       x_sb[:, bass.ds(t + i * (NT // NX), 1), :]).then_inc(stats_done, 1)
            dve.wait_ge(stats_done, NT)
            link(nc.vector.tensor_tensor(mean[:], stats[:, :, 1], stats[:, :, 4], ALU.add))
            link(nc.vector.tensor_scalar(mean[:], mean[:], 0.5, None, ALU.mult))
            link(nc.vector.tensor_tensor(tmp[:, 0, :], stats[:, :, 1], stats[:, :, 4], ALU.subtract))
            link(nc.vector.tensor_tensor(tmp[:, 0, :], tmp[:, 0, :], tmp[:, 0, :], ALU.mult))
            link(nc.vector.tensor_tensor(tmp[:, 1, :], stats[:, :, 2], stats[:, :, 5], ALU.add))
            link(nc.vector.tensor_scalar(tmp[:, 1, :], tmp[:, 1, :], 1.0 / D, EPS, ALU.mult, ALU.add))
            nc.vector.scalar_tensor_tensor(out=tmp[:, 2, :], in0=tmp[:, 0, :], scalar=0.25, in1=tmp[:, 1, :],
                                           op0=ALU.mult, op1=ALU.add).then_inc(var_ready, 1)
            dve.wait_ge(std_ready, 1)
            link(nc.vector.reciprocal(rstd[:], tmp[:, 3, :]))
            dve.wait_ge(weights_loaded, 16 * NW)
            link(nc.vector.tensor_copy(ident_b[:], ident[:]))

            def norm(n, s, first=False):
                if not first:
                    dve.wait_ge(xt_done, n * 2 - 2)
                for j in range(GT):
                    t = bass.ds(n * GT + j, 1)
                    ins = nc.vector.tensor_scalar(xn[s][:, j, :], x_sb[:, t, :], mean[:, t], rstd[:, t],
                                                  ALU.subtract, ALU.mult)
                ins.then_inc(xn_ready, 1)

            def rotate(n, j):
                t = n * GT + j
                tab = rope[:, bass.ds(t, 1), :]
                hd = DH // 2
                dve.wait_ge(qkv_out, past(t + 1))
                dve.wait_ge(rope_done, past(t))
                q2 = qk_s[j].rearrange("p (h d) -> p h d", d=hd)
                q4 = qk_s[j].rearrange("p (h a d) -> p h a d", a=2, d=hd)
                b4 = rb.rearrange("p (h a d) -> p h a d", a=2, d=hd)
                nc.vector.tensor_tensor(ra.rearrange("p (h d) -> p h d", d=hd), q2,
                                        tab[:, :, 0:hd].to_broadcast([P, 2 * QK // DH, hd]), ALU.mult)
                nc.vector.tensor_tensor(b4[:, :, 0, :], q4[:, :, 1, :],
                                        tab[:, :, 2 * hd:3 * hd].to_broadcast([P, QK // DH, hd]), ALU.mult)
                link(nc.vector.tensor_tensor(b4[:, :, 1, :], q4[:, :, 0, :],
                                             tab[:, :, hd:2 * hd].to_broadcast([P, QK // DH, hd]), ALU.mult))
                link(nc.vector.tensor_tensor(rq, ra, rb, ALU.add))
                if j < 2:
                    dve.wait_ge(pt_done, past(n * (2 * GT)))
                else:
                    dve.wait_ge(pt_done, past(t * 2 - 2))
                part = parts[j % 2]
                link(nc.vector.tensor_copy(part[:, 0, :], rq))
                link(nc.vector.tensor_tensor(ra, rq, part[:, 0, :], ALU.subtract))
                link(nc.vector.tensor_copy(part[:, 1, :], ra))
                nc.vector.tensor_tensor(part[:, 2, :], ra, part[:, 1, :], ALU.subtract).then_inc(rope_done, 1)

            def route(n):
                dve.wait_ge(qkv_out, past(n * GT + GT))
                dve.wait_ge(hit_ready, past(n))
                full = [P, GT, E]
                link(nc.vector.tensor_reduce(best, logit, AX.X, ALU.max))
                link(nc.vector.tensor_tensor(hit, logit, best.unsqueeze(2).to_broadcast(full), ALU.is_equal))
                link(nc.vector.tensor_tensor(hit, hit, rank[:].unsqueeze(1).to_broadcast(full), ALU.mult))
                link(nc.vector.tensor_reduce(best, hit, AX.X, ALU.max))
                dve.wait_ge(choice_ready, n)
                nc.vector.tensor_tensor(won, hit, best.unsqueeze(2).to_broadcast(full),
                                        ALU.is_equal).then_inc(hit_ready, 1)

            def expert(n, c):
                m = n * EC + c
                dve.wait_ge(relu_done, m + 1)
                dve.wait_ge(mask_done, past(m + 1))
                dve.wait_ge(squared, past(n * EC + max(c - 1, 0)))
                nc.vector.tensor_tensor(hid_m[c % 2], hid[c % 2], ps[:, 4, :], ALU.mult).then_inc(masked, 1)
                dve.wait_ge(squared, past(m + 1))
                dve.wait_ge(u_done, m + 1)
                if c == 0:
                    dve.wait_ge(wd_done, past(n * 2))
                nc.vector.tensor_tensor(inter[:, c, :], hid_q[c % 2], ps[:, 1 + 2 * (c % 2), :],
                                        ALU.mult).then_inc(inter_ready, 1)

            STEPS = GT * 5 + 4

            def group(n, s, has_next):
                rotate(n, 0)
                if has_next:
                    norm(n + 1, 1 - s)
                rotate(n, 1)
                route(n)
                expert(n, 0)
                rotate(n, 2)
                expert(n, 1)
                rotate(n, 3)
                expert(n, 2)
                expert(n, 3)

            assert count[0] == SETUP_STEPS
            norm(0, 0, first=True)
            with dve.Fori(0, NG // 2 - 1) as gp:
                base[0], count[0] = gp * (2 * STEPS) + SETUP_STEPS, 0
                for s in range(2):
                    group(gp * 2 + s, s, True)
                assert count[0] == 2 * STEPS
            base[0], count[0] = SETUP_STEPS + (NG - 2) * STEPS, 0
            group(NG - 2, 0, True)
            group(NG - 1, 1, False)

            dve.wait_ge(parts_stored, past(PSTORES * NG))
            dve.wait_ge(gate_ready, past(2 * NG))
            memset_ones()

            def reduce(t, head_slot, tile):
                for u in range(2):
                    dve.wait_ge(a_scored[u], t + 1)
                    nc.vector.tensor_reduce(most[head_slot][:, tile, u:u + 1], ps[:, 2 + 2 * u:4 + 2 * u, :], AX.XY,
                                            ALU.max).then_inc(a_reduced[u], 1)

            def cut_maxima(head, head_slot):
                for u in range(2):
                    dve.wait_ge(a_reduced[u], past(head * KB + KB))
                link(nc.vector.tensor_reduce(negm, most[head_slot], AX.X, ALU.max, negate=True))
                dve.wait_ge(mt_done, head)
                link(nc.vector.tensor_copy(mpart[:, 0:KB], negm))
                link(nc.vector.tensor_tensor(mres, negm, mpart[:, 0:KB], ALU.subtract))
                link(nc.vector.tensor_copy(mpart[:, KB:2 * KB], mres))
                nc.vector.tensor_tensor(mpart[:, 2 * KB:3 * KB], mres, mpart[:, KB:2 * KB],
                                        ALU.subtract).then_inc(mpart_ready, 1)

            def copy_maxima(head, head_slot, count_before):
                dve.wait_ge(mt_done, head + 1)
                if count_before is not None:
                    dve.wait_ge(shift_loaded[1 - head_slot], count_before)
                nc.vector.tensor_copy(mrow[0:NPART * KB, :],
                                      bank_b(6 + head_slot)[0:NPART * KB, 0:P]).then_inc(mrow_ready, 1)

            base[0], count[0] = SETUP_STEPS + NG * STEPS, 0
            for t in range(AHEAD):
                reduce(t, t // KB, t % KB)
                if t == KB - 1:
                    cut_maxima(0, 0)
            copy_maxima(0, 0, None)
            assert count[0] == 4

            def invert(s, n):
                dve.wait_ge(spread_in[s], past(n * 16))
                nc.vector.reciprocal(spread[s], spread[s]).then_inc(rec_ready[s], 1)

            def pair(pi, last_pair):
                for s in range(2):
                    for kb in range(KB):
                        g = pi * (2 * KB) + (s * KB + kb)
                        ahead = kb + AHEAD - KB
                        if kb == 4:
                            invert(1 - s, pi + s)
                        if not last_pair or (s == 0 and ahead < KB):
                            reduce(g + AHEAD, (s + 1 + ahead // KB) % 2, ahead % KB)
                        if not (last_pair and s == 1):
                            if ahead == KB - 1:
                                cut_maxima(pi * 2 + (s + 1), 1 - s)
                            if ahead == KB:
                                copy_maxima(pi * 2 + (s + 1), 1 - s, (pi + 1) * 16)
                    dve.wait_ge(pv_done[1], past(pi * KB + (s + 1) * NB2))
                    dve.wait_ge(spread_in[s], past(pi * 16))
                    dve.wait_ge(o_stored[s], past(pi * (16 * QT)))
                    nc.vector.tensor_copy(osb[s], ps[:, 6 + s, :]).then_inc(o_out[s], 1)

            with dve.Fori(0, NP - 1) as pi:
                base[0], count[0] = pi * 8 + (SETUP_STEPS + NG * STEPS + 4), 0
                pair(pi, False)
                assert count[0] == 8
            base[0], count[0] = (NP - 1) * 8 + (SETUP_STEPS + NG * STEPS + 4), 0
            pair(NP - 1, True)

            invert(1, NP)
            base[0], count[0] = base[0] + count[0], 0
            for b in range(B):
                if b == B - 1:
                    dve.wait_ge(chunk_loaded, 16 * 2 * NC)
                    for t in range(QT):
                        sl = onum[:, NC - 1, t * W:(t + 1) * W]
                        nc.vector.tensor_tensor(sl, sl, orec[:, t * W:(t + 1) * W], ALU.mult).then_inc(normed, 1)
                for i in range(ENDT):
                    n = b * ENDT + i
                    dve.wait_ge(proj_done, n + 1)
                    if n >= 2:
                        dve.wait_ge(res_stored[i % 2], 16 * (n // 2))
                    link(nc.vector.tensor_tensor(res[i % 2], ps[:, i % 4, :].rearrange("p (t d) -> p t d", d=D),
                                                 gate[:, 2 * n:2 * n + 2, :], ALU.mult))
                    nc.vector.tensor_tensor(res[i % 2], res[i % 2], x_sb[:, 2 * n:2 * n + 2, :],
                                            ALU.add).then_inc(res_ready[i % 2], 1)

        @block.gpsimd
        def _(pool):
            for counter in from_one:
                pool.sem_inc(counter, 1)
            pool.sem_inc(counters_set, 1)
            with pool.Fori(0, NG) as n:
                pool.wait_ge(hit_ready, past(n + 1))
                pool.wait_ge(mask_done, past(n * EC))
                many = won.unsqueeze(3).to_broadcast([P, GT, E, DE])
                nc.gpsimd.tensor_tensor(choice, many, many, ALU.mult).then_inc(choice_ready, 1)

            def stage(b, j, s, pi):
                pool.wait_ge(o_out[s], past(pi))
                h = j * 2 + s
                pool.wait_ge(consts_ready, 2)
                nc.gpsimd.tensor_copy(vst[s][:, :, 1:1 + DH],
                                      v_sb[:, b * KB:(b + 1) * KB, bass.ds(h * DH, DH)]).then_inc(v_staged[s], 1)

            def weigh(m):
                pool.wait_ge(chunk_loaded, 16 * 2 * (m + 1))
                nc.gpsimd.tensor_tensor(onum[:, m, :], onum[:, m, :], orec, ALU.mult).then_inc(chunk_weighed, 1)

            pool.wait_ge(consts_ready, 2)
            for m in range(NC):
                b, first = divmod(m * CP, H // 2)
                with pool.Fori(first, first + CP) as j:
                    for s in range(2):
                        stage(b, j, s, j + b * (H // 2))
                if m:
                    weigh(m - 1)
        @block.tensor
        def _(pe):
            pe.wait_ge(counters_set, 1)
            pe.wait_ge(weights_loaded, 16 * NW)
            pe.wait_ge(dve_step, SETUP_STEPS)

            def transpose_x(n, s):
                pe.wait_ge(xn_ready, n + 1)
                for j in range(GT):
                    for k in range(KC):
                        last = nc.tensor.transpose(ps[:, 6 + j // 2, (2 * k + j % 2) * P:(2 * k + j % 2 + 1) * P],
                                                   xn[s][:, j, k * P:(k + 1) * P], ident[:])
                    if j % 2:
                        last.then_inc(xt_done, 1)

            def group(n, s, has_next):
                pe.wait_ge(xt_out, n * 2 + 2)
                for j in range(GT):
                    o = 2 * (j % 2)
                    if j < 2:
                        pe.wait_ge(inter_ready, past(n * EC))
                    else:
                        pe.wait_ge(qkv_out, past(n * GT + j - 1))
                    for k in range(KC):
                        xt = xnT[s][:, k, j * P:(j + 1) * P]
                        nc.tensor.matmul(ps[:, o, :], xt, w_sb[:, k, 0:QK], start=(k == 0), stop=(k == KC - 1))
                        last = nc.tensor.matmul(ps[:, o + 1, 0:VG], xt, w_sb[:, k, QK:QK + VG],
                                                start=(k == 0), stop=(k == KC - 1))
                    last.then_inc(qkv_done, 1)
                pe.wait_ge(gate_ready, past(n * 2))
                if has_next:
                    transpose_x(n + 1, 1 - s)
                for c in range(EC):
                    m = n * EC + c
                    o = 2 * (c % 2)
                    if c < 2:
                        pe.wait_ge(qkv_out, past(n * GT + (c + 3)))
                    else:
                        pe.wait_ge(inter_ready, past(m - 1))
                    for k in range(KC):
                        last = nc.tensor.matmul(ps[:, o, :], wg_sb[:, k, c * P:(c + 1) * P], xnT[s][:, k, :],
                                                start=(k == 0), stop=(k == KC - 1))
                    last.then_inc(g_done, 1)
                    if c == 0:
                        pe.wait_ge(choice_ready, n + 1)
                    pe.wait_ge(masked, past(m))
                    for j in range(GT):
                        last = nc.tensor.matmul(ps[:, 4, j * P:(j + 1) * P],
                                                choice[:, j, :, :].rearrange("p e d -> p (e d)")[:, c * P:(c + 1) * P],
                                                ident_b[:], start=True, stop=True)
                    last.then_inc(mask_done, 1)
                    for i in range(2):
                        if i == 0:
                            pe.wait_ge(rope_done, past(m + 1))
                        else:
                            for k in range(KC):
                                last = nc.tensor.matmul(ps[:, o + 1, :], wu_sb[:, k, c * P:(c + 1) * P],
                                                        xnT[s][:, k, :], start=(k == 0), stop=(k == KC - 1))
                            last.then_inc(u_done, 1)
                        pe.wait_ge(pt_out, past(m * 2 + i))
                        for q in range(HM):
                            a, kc = divmod(i * HM + q, 2 * KC)
                            last = nc.tensor.transpose(bank_b(5)[:, q * P:(q + 1) * P],
                                                       parts[c % 2][:, a, kc * P:(kc + 1) * P], ident_b[:])
                        last.then_inc(pt_done, 1)
                pe.wait_ge(inter_ready, past(n * EC + EC))
                if has_next:
                    pe.wait_ge(xt_out, n * 2 + 4)
                for j in range(GT):
                    for c in range(EC):
                        last = nc.tensor.matmul(ps[:, 6 + j // 2, (j % 2) * D:(j % 2 + 1) * D],
                                                inter[:, c, j * P:(j + 1) * P], wd_sb[:, c, :],
                                                start=(c == 0), stop=(c == EC - 1))
                    if j % 2:
                        last.then_inc(wd_done, 1)

            transpose_x(0, 0)
            with pe.Fori(0, NG // 2 - 1) as gp:
                for s in range(2):
                    group(gp * 2 + s, s, True)
            group(NG - 2, 0, True)
            group(NG - 1, 1, False)

            pe.wait_ge(pt_out, past(2 * NT))
            pe.wait_ge(gate_ready, past(2 * NG))
            def score_a(t, head_slot, tile, u):
                pe.wait_ge(a_reduced[u], past(t))
                for c in range(2):
                    last = nc.tensor.matmul(ps[:, 2 + 2 * u + c, :], qa[head_slot][0:KR, tile * P:(tile + 1) * P],
                                            ka[head_slot][0:KR, (2 * u + c) * W:(2 * u + c + 1) * W],
                                            start=True, stop=True)
                last.then_inc(a_scored[u], 1)

            def transpose_maxima(head, head_slot):
                pe.wait_ge(mpart_ready, head + 1)
                nc.tensor.transpose(bank_b(6 + head_slot)[:, 0:P], mpart, ident_b[:]).then_inc(mt_done, 1)

            def score(s, kb, c, n):
                pe.wait_ge(exp_done[c % 2], past(n))
                nc.tensor.matmul(ps[:, c % 2, :], kst[s][0:KS, kb * P:(kb + 1) * P],
                                 qst[s][0:KS, c * W:(c + 1) * W], start=True, stop=True).then_inc(scored[c % 2], 1)

            for t in range(AHEAD):
                if t % KB == 0:
                    pe.wait_ge(a_loaded[t // KB], 16 * LOADS)
                for u in range(2):
                    score_a(t, t // KB, t % KB, u)
            transpose_maxima(0, 0)
            pe.wait_ge(loaded[0], 16 * LOADS)
            pe.wait_ge(shift_loaded[0], 16)
            for c in range(QT):
                score(0, 0, c, c // 2)

            def pair(pi, last_pair):
                for s in range(2):
                    for kb in range(KB):
                        g = pi * (2 * KB) + (s * KB + kb)
                        ahead = kb + AHEAD - KB
                        with_a = not last_pair or (s == 0 and ahead < KB)
                        with_b = not (last_pair and s == 1 and kb == KB - 1)
                        a_slot = (s + 1 + ahead // KB) % 2
                        b_slot = s if kb < KB - 1 else 1 - s
                        used = pi * (4 * KB) + (s * 2 * KB + kb * 2 + 2)
                        if kb == KB - 1 and with_b:
                            pe.wait_ge(loaded[b_slot], (pi + 1 + s) * (16 * LOADS))
                            pe.wait_ge(shift_loaded[b_slot], (pi + 1 + s) * 16)
                        if with_a and ahead % KB == 0:
                            pe.wait_ge(a_loaded[a_slot], (pi + 2) * (16 * LOADS))
                        if with_b:
                            for c in range(2):
                                score(b_slot, (kb + 1) % KB, c, used)
                        if with_a:
                            for u in range(2):
                                score_a(g + AHEAD, a_slot, ahead % KB, u)
                        if with_b:
                            for c in range(2, QT):
                                score(b_slot, (kb + 1) % KB, c, used + 1)
                        if ahead == KB and not (last_pair and s == 1):
                            transpose_maxima(pi * 2 + (s + 1), 1 - s)
                        if kb == 0:
                            pe.wait_ge(v_staged[s], pi + 1)
                            pe.wait_ge(o_out[s], past(pi))
                            pe.wait_ge(mrow_ready, pi * 2 + (s + 1))
                        for i in range(2):
                            pe.wait_ge(exp_done[i], past(used))
                        for c in range(QT):
                            last = nc.tensor.matmul(ps[32 * c:32 * (c + 1), 6 + s, :], vst[s][:, kb, :],
                                                    prob[kb % 2][:, c * W:(c + 1) * W],
                                                    start=(kb == 0), stop=(kb == KB - 1))
                        last.then_inc(pv_done[kb % 2], 1)

            with pe.Fori(0, NP - 1) as pi:
                pair(pi, False)
            pair(NP - 1, True)

            for b in range(B):
                for i in range(ENDT):
                    n = b * ENDT + i
                    if i == 0:
                        pe.wait_ge(chunk_weighed, min(KC * (b + 1), NC - 1))
                        pe.wait_ge(a_reduced[0], past(NH * KB))
                    if b == B - 1:
                        pe.wait_ge(normed, i // 2 + 1)
                    if n >= 4:
                        pe.wait_ge(res_ready[i % 2], n // 2 - 1)
                    for t in range(2):
                        for k in range(KC):
                            last = nc.tensor.matmul(ps[:, i % 4, t * D:(t + 1) * D],
                                                    onum[:, b * KC + k, (2 * i + t) * P:(2 * i + t + 1) * P], wo_sb[:, k, :],
                                                    start=(k == 0), stop=(k == KC - 1))
                    last.then_inc(proj_done, 1)


def kernel(L0_attn_x, L0_attn_w_qkv, L0_attn_w_out, L0_ffn_gate_w, L0_ffn_wg, L0_ffn_wu, L0_ffn_wd):
    import numpy as np
    import concourse.bacc as bacc
    from concourse import mybir
    from concourse.bass_utils import run_bass_kernel_spmd

    def rows(a):
        return np.ascontiguousarray(a.reshape(-1, 128, a.shape[-1]).transpose(1, 0, 2))

    x = np.ascontiguousarray(L0_attn_x)
    e, d, f = L0_ffn_wg.shape
    length, half = x.shape[1], 8
    inv = np.float32(1.0) / np.float32(10000.0) ** (np.arange(half, dtype=np.float32) / np.float32(half))
    ang = np.arange(length, dtype=np.float32)[:, None] * inv[None, :].astype(np.float32)
    table = np.concatenate([np.cos(ang), np.sin(ang), -np.sin(ang)], axis=-1).astype(np.float32)
    arrays = {
        "x": x,
        "w": rows(np.concatenate([np.asarray(L0_attn_w_qkv), np.asarray(L0_ffn_gate_w)], axis=0).T),
        "wout": rows(np.asarray(L0_attn_w_out).T),
        "wg": rows(np.asarray(L0_ffn_wg).transpose(1, 0, 2).reshape(d, e * f)),
        "wu": rows(np.asarray(L0_ffn_wu).transpose(1, 0, 2).reshape(d, e * f)),
        "wd": rows(np.asarray(L0_ffn_wd).reshape(e * f, d)),
        "rope": np.tile(rows(table), (1, x.shape[0], 1)),
        "ident": np.eye(128, dtype=np.float32),
        "rank": np.tile(np.arange(e, 0, -1, dtype=np.float32), (128, 1)),
    }
    nc = bacc.Bacc("TRN2", target_bir_lowering=False, num_devices=1)
    args, feed = [], {}
    for name, a in arrays.items():
        feed[f"in_{name}"] = a
        args.append(nc.dram_tensor(f"in_{name}", a.shape, mybir.dt.from_np(a.dtype), kind="ExternalInput").ap())
    args.append(nc.dram_tensor("out", x.shape, mybir.dt.float32, kind="ExternalOutput").ap())
    layer_kernel(nc, *args)
    got = run_bass_kernel_spmd(nc, [feed], core_ids=[0])
    return got.results[0]["out"]
```

```python
import concourse.bass as bass
from concourse import mybir
from contextlib import ExitStack


def layer_kernel(nc, x_in, w_in, wout_in, wg_in, wu_in, wd_in, rope_in, ident_in, rank_in, out):
    F32, BF16 = mybir.dt.float32, mybir.dt.bfloat16
    ALU, ACT, AX = mybir.AluOpType, mybir.ActivationFunctionType, mybir.AxisListType

    B, L, D = 2, 2048, 256
    H, DH = 16, 16
    E, DE = 8, 64
    P = 128
    NT = B * L // P
    GT = 4
    NG = NT // GT
    W = GT * P
    KC = D // P
    XCUT = (0, GT, 2 * GT, 4 * GT, NT)
    EARLY = NG // B
    EC = E * DE // P
    EP = E // EC
    QK = 2 * D
    VG = D + E
    NPART = 3
    QPARTS = (0, 0, 0, 1, 1, 1, 2)
    KPARTS = (0, 1, 2, 0, 1, 2, 0)
    KR = DH * len(QPARTS)
    KS = KR + NPART
    NM = NPART * 2 * KC
    HM = NM // 2
    NH = B * H
    KB = L // P
    QT = L // W
    SCALE = DH ** -0.5
    EPS = 1e-5
    NC = B * KC
    NR = 4
    CP = NH // 2 // NC
    LOADS = 6
    CUTS = 5
    COPY_STEP = 3
    AHEAD = KB + 5

    x_v = x_in.rearrange("b (t p) d -> p (b t) d", p=P)
    out_v = out.rearrange("b (t p) d -> p (b t) d", p=P)

    ctx = ExitStack()
    with ctx:
        def sb(name, shape, dt=F32):
            return ctx.enter_context(nc.sbuf_tensor(name, shape, dt))

        def sem(name):
            return ctx.enter_context(nc.semaphore(name))

        parts_d = nc.dram_tensor("parts_d", (NPART, 2, B * D, L), BF16, kind="Internal").ap()
        onum_d = nc.dram_tensor("onum_d", (B * D, L), F32, kind="Internal").ap()
        orec_d = nc.dram_tensor("orec_d", (NH, L), F32, kind="Internal").ap()

        x_sb = sb("x_sb", [P, NT, D])
        v_sb = sb("v_sb", [P, NT, D])
        gate = sb("gate", [P, NT, D])
        wo_sb = sb("wo_sb", [P, KC, D])
        rope = sb("rope", [P, NT, 3 * DH // 2])
        ident = sb("ident", [P, P])
        ident_b = sb("ident_b", [P, P], BF16)
        rank = sb("rank", [P, E])
        stats = sb("stats", [P, NT, 6])
        mean = sb("mean", [P, NT])
        rstd = sb("rstd", [P, NT])
        tmp = sb("tmp", [P, 4, NT])

        ARENA = 26760
        arena = sb("arena", [P, ARENA])
        at = [0]

        def cut(shape, dt=F32):
            n = 1
            for s in shape:
                n *= s
            words = n * (2 if dt == BF16 else 4) // 4
            flat = arena[:, at[0]:at[0] + words]
            at[0] += words
            assert at[0] <= ARENA
            if dt == BF16:
                flat = flat.bitcast(BF16)
            if len(shape) == 1:
                return flat
            names = "abcd"[:len(shape)]
            return flat.rearrange(f"p ({' '.join(names)}) -> p {' '.join(names)}", **dict(zip(names, shape)))

        w_sb = cut([KC, QK + VG])
        wg_sb = cut([KC, E * DE])
        wu_sb = cut([KC, E * DE])
        wd_sb = cut([EC, D])
        xn = [cut([GT, D]) for _ in range(2)]
        xnT = [cut([KC, W]) for _ in range(2)]
        qk_s = [cut([QK]) for _ in range(GT)]
        ra = [cut([QK]) for _ in range(2)]
        rb, rq = cut([QK]), cut([QK])
        parts = [cut([NPART, QK], BF16) for _ in range(2)]
        pst = cut([NM, W], BF16)
        hid = [cut([W]) for _ in range(2)]
        hid_m = [cut([W]) for _ in range(2)]
        hid_q = [cut([W]) for _ in range(2)]
        inter = cut([EC, W])
        logit = cut([GT, E])
        hit = cut([GT, E])
        won = cut([GT, E], BF16)
        best = cut([GT])
        assert at[0] <= ARENA
        GROUPS_END = at[0]
        qa, ka = [cut([L], BF16)], [cut([L], BF16)]
        qst, kst = [cut([L], BF16)], [cut([L], BF16)]
        most = [cut([KB, 2])]
        at[0] = 0
        negm = cut([KB])
        mres = cut([KB])
        mpart = cut([P], BF16)
        mrow = cut([P], BF16)
        spread = [cut([L // P]) for _ in range(2)]
        stacks_at = at[0]
        res = [cut([2, D]) for _ in range(NR)]
        at[0] = stacks_at
        for stack in (qa, ka, qst, kst):
            stack.append(cut([L], BF16))
        most.append(cut([KB, 2]))
        prob = [cut([L]) for _ in range(2)]
        vst = [cut([KB, 32]) for _ in range(2)]
        osb = [cut([W]) for _ in range(2)]
        onum = cut([NC, L])
        orec = cut([L])
        assert at[0] <= GROUPS_END

        ps = ctx.enter_context(nc.psum_tensor("ps", [P, 8, 512], F32))

        def bank_b(i):
            return ps[:, i, :].bitcast(BF16)

        x_loaded = [sem(f"x_loaded{i}") for i in range(len(XCUT) - 1)]
        first_loaded = sem("first_loaded")
        weights_loaded = sem("weights_loaded")
        stats_done = sem("stats_done")
        dve_step = sem("dve_step")
        var_ready = sem("var_ready")
        std_ready = sem("std_ready")
        identity_ready = sem("identity_ready")
        centered = sem("centered")
        xn_ready = sem("xn_ready")
        xt_done = sem("xt_done")
        xt_out = sem("xt_out")
        qkv_done = sem("qkv_done")
        qkv_out = sem("qkv_out")
        mid_ready = sem("mid_ready")
        rope_done = sem("rope_done")
        pt_done = sem("pt_done")
        pt_out = sem("pt_out")
        parts_stored = sem("parts_stored")
        hit_ready = sem("hit_ready")
        g_done = sem("g_done")
        mask_done = sem("mask_done")
        u_done = sem("u_done")
        relu_done = sem("relu_done")
        masked = sem("masked")
        squared = sem("squared")
        inter_ready = sem("inter_ready")
        wd_done = sem("wd_done")
        gate_ready = sem("gate_ready")
        first_ones = sem("first_ones")
        consts_ready = sem("consts_ready")
        a_loaded = [sem(f"a_loaded{i}") for i in range(2)]
        a_scored = [sem(f"a_scored{i}") for i in range(2)]
        a_reduced = [sem(f"a_reduced{i}") for i in range(2)]
        mpart_ready = sem("mpart_ready")
        mt_done = sem("mt_done")
        mrow_ready = sem("mrow_ready")
        shift_loaded = [sem(f"shift_loaded{i}") for i in range(2)]
        loaded = [sem(f"loaded{i}") for i in range(2)]
        scored = [sem(f"scored{i}") for i in range(2)]
        exp_done = [sem(f"exp_done{i}") for i in range(2)]
        pv_done = [sem(f"pv_done{i}") for i in range(2)]
        v_staged = [sem(f"v_staged{i}") for i in range(2)]
        o_out = [sem(f"o_out{i}") for i in range(2)]
        o_stored = [sem(f"o_stored{i}") for i in range(2)]
        spread_in = [sem(f"spread_in{i}") for i in range(2)]
        rec_ready = [sem(f"rec_ready{i}") for i in range(2)]
        rec_stored = [sem(f"rec_stored{i}") for i in range(2)]
        chunk_loaded = sem("chunk_loaded")
        chunk_weighed = sem("chunk_weighed")
        normed = sem("normed")
        proj_done = sem("proj_done")
        res_ready = [sem(f"res_ready{i}") for i in range(NR)]
        res_stored = [sem(f"res_stored{i}") for i in range(NR)]

        PSTORES = 16 * NPART * 2
        NW = 6
        NP = NH // 2
        NB2 = KB // 2
        ENDT = KB // 2
        SETUP_STEPS = 14

        from_one = [rope_done, hit_ready, masked, parts_stored, squared, inter_ready, gate_ready, pt_done, qkv_out,
                    pt_out, wd_done, mask_done, *pv_done, *exp_done, *o_out, *o_stored, *a_reduced,
                    *spread_in, *rec_stored, mid_ready]

        counters_set = sem("counters_set")

        def past(n):
            return n + 1

        block = ctx.enter_context(nc.Block())

        def stack_loads(eng, head, qstack, kstack, done):
            rows = bass.ds(head * DH, DH)
            for qk, stack, order in ((0, qstack, QPARTS), (1, kstack, KPARTS)):
                for i in range(2):
                    if qk == 0:
                        src = parts_d[order[3 * i], qk, rows, :].unsqueeze(0).to_broadcast([3, DH, L])
                    else:
                        src = parts_d[:, qk, rows, :]
                    eng.dma_start(stack[3 * DH * i:3 * DH * (i + 1), :], src).then_inc(done, 16)
                eng.dma_start(stack[6 * DH:7 * DH, :], parts_d[order[6], qk, rows, :]).then_inc(done, 16)

        @block.sync
        def _(sp):
            for i, (lo, hi) in enumerate(zip(XCUT, XCUT[1:])):
                sp.dma_start(x_sb[:, lo:hi, :], x_v[:, lo:hi, :]).then_inc(x_loaded[i], 16)

            sp.wait_ge(counters_set, 1)
            for b in range(B):
                with sp.Fori(0, QT) as t:
                    sp.wait_ge(pt_out, past(t * (2 * GT) + (b * QT + 1) * 2 * GT))
                    for m in range(NPART * 2):
                        a, qk = divmod(m, 2)
                        sp.dma_start(parts_d[a, qk, b * D:(b + 1) * D, bass.ds(t * W, W)].rearrange(
                            "(c p) t -> p c t", p=P), pst[:, m * KC:(m + 1) * KC, :]).then_inc(parts_stored, 16)
                sp.wait_ge(parts_stored, past(PSTORES * QT * (b + 1)))
                if b == 0:
                    sp.wait_ge(first_ones, 1)
                    stack_loads(sp, 0, qa[0], ka[0], a_loaded[0])
                    stack_loads(sp, 0, qst[0], kst[0], loaded[0])
            sp.wait_ge(u_done, NT)

            def load_a(head, s):
                stack_loads(sp, head, qa[s], ka[s], a_loaded[s])

            def load(head, s):
                stack_loads(sp, head, qst[s], kst[s], loaded[s])

            def shift(head, s):
                sp.wait_ge(mrow_ready, head + 1)
                sp.dma_start(qst[s][KR:KS, :], mrow[0:NPART * KB, :]).then_inc(shift_loaded[s], 16)

            def store(head, s, pi):
                sp.wait_ge(o_out[s], past(pi + 1))
                sp.wait_ge(rec_stored[s], past(pi * 16))
                sp.dma_start(spread[s], osb[s][0:P:32, :]).then_inc(spread_in[s], 16)
                for c in range(QT):
                    sp.dma_start(onum_d[bass.ds(head * DH, DH), c * W:(c + 1) * W],
                                 osb[s][32 * c + 1:32 * c + 1 + DH, :]).then_inc(o_stored[s], 16)
                sp.wait_ge(rec_ready[s], pi + 1 + s)
                sp.dma_start(orec_d[bass.ds(head, 1), :].rearrange("h (c t) -> (h c) t", t=L // P),
                             spread[s]).then_inc(rec_stored[s], 16)

            def load_chunk(m, p0, p1):
                rows = slice(p0 * 2 * DH, p1 * 2 * DH)
                heads = slice((m * CP + p0) * 2, (m * CP + p1) * 2)
                if m:
                    sp.wait_ge(chunk_weighed, m)
                for s in range(2):
                    sp.wait_ge(o_stored[s], past(16 * QT * (m * CP + p1)))
                sp.dma_start(onum[rows, m, :], onum_d[m * P + rows.start:m * P + rows.stop, :]).then_inc(chunk_loaded, 16)
                for s in range(2):
                    sp.wait_ge(rec_stored[s], past(16 * (m * CP + p1)))
                src = orec_d[heads, :].unsqueeze(1).to_broadcast([(p1 - p0) * 2, DH, L])
                sp.dma_start(orec[rows, :], src).then_inc(chunk_loaded, 16)

            load_a(1, 1)
            shift(0, 0)
            sp.wait_ge(consts_ready, 3)
            load(1, 1)
            sp.wait_ge(a_scored[1], KB)
            load_a(2, 0)

            def pair(pi):
                for s in range(2):
                    n = pi * 2 + s
                    known = isinstance(n, int)
                    if not known or n + 3 < NH:
                        sp.wait_ge(a_scored[1], n * KB + 2 * KB)
                        load_a(n + 3, 1 - s)
                    if not known or n + 1 < NH:
                        shift(n + 1, 1 - s)
                    if not known or n + 2 < NH:
                        sp.wait_ge(scored[1], n * (2 * KB) + 2 * KB)
                        load(n + 2, s)
                    store(n, s, pi)

            for m in range(NC):
                peeled = 2 * (m == NC - 1)
                with sp.Fori(m * CP, (m + 1) * CP - peeled) as pi:
                    pair(pi)
                if not peeled:
                    load_chunk(m, 0, CP)
            pair(NP - 2)
            load_chunk(NC - 1, 0, CP - 1)
            pair(NP - 1)
            load_chunk(NC - 1, CP - 1, CP)

        @block.scalar
        def _(act):
            for dst, src in ((ident[:], ident_in), (w_sb, w_in)):
                act.dma_start(dst, src).then_inc(first_loaded, 16)
            for dst, src in ((rope[:], rope_in), (rank[:], rank_in), (wg_sb, wg_in), (wu_sb, wu_in), (wd_sb, wd_in),
                             (wo_sb[:], wout_in)):
                act.dma_start(dst, src).then_inc(weights_loaded, 16)

            act.wait_ge(counters_set, 1)
            act.wait_ge(var_ready, 1)
            nc.scalar.activation(tmp[:, 3, 0:GT], tmp[:, 2, 0:GT], ACT.Sqrt).then_inc(std_ready, 1)

            def xt_copy(n, s):
                for i in range(2):
                    act.wait_ge(xt_done, n * 2 + (i + 1))
                    nc.scalar.copy(xnT[s][:, :, i * 2 * P:(i + 1) * 2 * P],
                                   ps[:, i, :].rearrange("p (k t) -> p k t", k=KC)).then_inc(xt_out, 1)

            def group(n, s, has_next):
                act.wait_ge(rope_done, past(n * GT))
                act.wait_ge(hit_ready, past(n))
                for j in range(GT):
                    o = 2 * (j % 2)
                    act.wait_ge(qkv_done, n * GT + (j + 1))
                    nc.scalar.copy(qk_s[j], ps[:, o, :])
                    nc.scalar.copy(v_sb[:, bass.ds(n * GT + j, 1), :], ps[:, o + 1, 0:D].unsqueeze(1))
                    nc.scalar.copy(logit[:, j, :], ps[:, o + 1, D:VG]).then_inc(qkv_out, 1)
                for c in range(EC):
                    act.wait_ge(g_done, n * EC + (c + 1))
                    act.wait_ge(masked, past(n * EC + max(c - 1, 0)))
                    nc.scalar.activation(hid[c % 2], ps[:, 2 * (c % 2), :], ACT.Relu).then_inc(relu_done, 1)
                    for i in range(2):
                        if c == 0 and i == 0:
                            act.wait_ge(parts_stored, past(n * PSTORES))
                        act.wait_ge(pt_done, past((n * GT + c) * 2 + i + 1))
                        nc.scalar.copy(pst[:, i * HM:(i + 1) * HM, c * P:(c + 1) * P],
                                       bank_b(5)[:, 0:HM * P].rearrange("p (m t) -> p m t", m=HM)).then_inc(pt_out, 1)
                    act.wait_ge(masked, past(n * EC + (c + 1)))
                    act.wait_ge(inter_ready, past(n * EC + max(c - 1, 0)))
                    nc.scalar.activation(hid_q[c % 2], hid_m[c % 2], ACT.Square).then_inc(squared, 1)
                if has_next:
                    xt_copy(n + 1, 1 - s)
                for i in range(2):
                    act.wait_ge(wd_done, past(n * 2 + (i + 1)))
                    nc.scalar.activation(gate[:, bass.ds(n * GT + 2 * i, 2), :],
                                         ps[:, 6 + i, :].rearrange("p (t d) -> p t d", d=D),
                                         ACT.Silu).then_inc(gate_ready, 1)

            xt_copy(0, 0)
            act.wait_ge(var_ready, 2)
            nc.scalar.activation(tmp[:, 3, GT:NT], tmp[:, 2, GT:NT], ACT.Sqrt).then_inc(std_ready, 1)
            with act.Fori(0, NG // 2 - 1) as gp:
                for s in range(2):
                    group(gp * 2 + s, s, True)
            group(NG - 2, 0, True)
            group(NG - 1, 1, False)

            with act.Fori(0, NP // 2) as p2:
                for h in range(4):
                    for kb in range(KB):
                        act.wait_ge(pv_done[kb % 2], past(p2 * (2 * KB) + (h * NB2 + kb // 2)))
                        for c in range(QT):
                            act.wait_ge(scored[c % 2], p2 * (8 * KB) + (h * 2 * KB + kb * 2 + c // 2 + 1))
                            nc.scalar.activation(prob[kb % 2][:, c * W:(c + 1) * W], ps[:, c % 2, :], ACT.Exp,
                                                 scale=SCALE).then_inc(exp_done[c % 2], 1)

            for b in range(B):
                for i in range(ENDT):
                    n = b * ENDT + i
                    act.wait_ge(res_ready[n % NR], n // NR + 1)
                    act.dma_start(out_v[:, 2 * n:2 * n + 2, :], res[n % NR]).then_inc(res_stored[n % NR], 16)
            for i in range(NR):
                act.wait_ge(res_stored[i], 16 * B * ENDT // NR)

        @block.vector
        def _(dve):
            base, count = [0], [0]

            def link(ins):
                count[0] += 1
                ins.then_inc(dve_step, 1)
                dve.wait_ge(dve_step, base[0] + count[0])

            def moments(k, pieces):
                ts = slice(XCUT[pieces[0]], XCUT[pieces[-1] + 1])
                for i in pieces:
                    dve.wait_ge(x_loaded[i], 16)
                    for t in range(XCUT[i], XCUT[i + 1]):
                        nc.vector.bn_stats(stats[:, t, :], x_sb[:, t, :]).then_inc(stats_done, 1)
                dve.wait_ge(stats_done, ts.stop)
                link(nc.vector.tensor_tensor(mean[:, ts], stats[:, ts, 1], stats[:, ts, 4], ALU.add))
                link(nc.vector.tensor_scalar(mean[:, ts], mean[:, ts], 0.5, None, ALU.mult))
                link(nc.vector.tensor_tensor(tmp[:, 0, ts], stats[:, ts, 1], stats[:, ts, 4], ALU.subtract))
                link(nc.vector.tensor_tensor(tmp[:, 0, ts], tmp[:, 0, ts], tmp[:, 0, ts], ALU.mult))
                link(nc.vector.tensor_tensor(tmp[:, 1, ts], stats[:, ts, 2], stats[:, ts, 5], ALU.add))
                link(nc.vector.tensor_scalar(tmp[:, 1, ts], tmp[:, 1, ts], 1.0 / D, EPS, ALU.mult, ALU.add))
                nc.vector.scalar_tensor_tensor(out=tmp[:, 2, ts], in0=tmp[:, 0, ts], scalar=0.25, in1=tmp[:, 1, ts],
                                               op0=ALU.mult, op1=ALU.add).then_inc(var_ready, 1)
                dve.wait_ge(std_ready, k + 1)
                link(nc.vector.reciprocal(rstd[:, ts], tmp[:, 3, ts]))

            dve.wait_ge(counters_set, 1)
            nc.vector.memset(kst[0][96:KS, :], 1.0).then_inc(first_ones, 1)
            dve.wait_ge(first_loaded, 16 * 2)
            nc.vector.tensor_copy(ident_b[:], ident[:]).then_inc(identity_ready, 1)
            moments(0, (0,))
            for j in range(GT):
                ins = nc.vector.tensor_scalar(xn[0][:, j, :], x_sb[:, j, :], mean[:, j:j + 1], rstd[:, j:j + 1],
                                              ALU.subtract, ALU.mult)
            ins.then_inc(xn_ready, 1)
            moments(1, (1, 2, 3))
            dve.wait_ge(weights_loaded, 16 * NW)

            def rotate(n, j):
                t = n * GT + j
                tab = rope[:, bass.ds(t, 1), :]
                hd = DH // 2
                dve.wait_ge(qkv_out, past(t + 1))
                dve.wait_ge(mid_ready, past(t))
                dve.wait_ge(rope_done, past(t - 1 if j else t))
                q2 = qk_s[j].rearrange("p (h d) -> p h d", d=hd)
                q4 = qk_s[j].rearrange("p (h a d) -> p h a d", a=2, d=hd)
                b4 = rb.rearrange("p (h a d) -> p h a d", a=2, d=hd)
                nc.vector.tensor_tensor(ra[j % 2].rearrange("p (h d) -> p h d", d=hd), q2,
                                        tab[:, :, 0:hd].to_broadcast([P, 2 * QK // DH, hd]), ALU.mult)
                nc.vector.tensor_tensor(b4[:, :, 0, :], q4[:, :, 1, :],
                                        tab[:, :, 2 * hd:3 * hd].to_broadcast([P, QK // DH, hd]), ALU.mult)
                link(nc.vector.tensor_tensor(b4[:, :, 1, :], q4[:, :, 0, :],
                                             tab[:, :, hd:2 * hd].to_broadcast([P, QK // DH, hd]), ALU.mult))
                link(nc.vector.tensor_tensor(rq, ra[j % 2], rb, ALU.add))
                if j < 2:
                    dve.wait_ge(pt_done, past(n * (2 * GT)))
                else:
                    dve.wait_ge(pt_done, past(t * 2 - 2))
                part = parts[j % 2]
                link(nc.vector.tensor_copy(part[:, 0, :], rq))
                link(nc.vector.tensor_tensor(ra[j % 2], rq, part[:, 0, :], ALU.subtract))
                nc.vector.tensor_copy(part[:, 1, :], ra[j % 2]).then_inc(mid_ready, 1)

            def route(n):
                dve.wait_ge(qkv_out, past(n * GT + GT))
                dve.wait_ge(hit_ready, past(n))
                full = [P, GT, E]
                link(nc.vector.tensor_reduce(best, logit, AX.X, ALU.max))
                link(nc.vector.tensor_tensor(hit, logit, best.unsqueeze(2).to_broadcast(full), ALU.is_equal))
                link(nc.vector.tensor_tensor(hit, hit, rank[:].unsqueeze(1).to_broadcast(full), ALU.mult))
                link(nc.vector.tensor_reduce(best, hit, AX.X, ALU.max))
                dve.wait_ge(mask_done, past(n * EC))
                nc.vector.tensor_tensor(won, hit, best.unsqueeze(2).to_broadcast(full),
                                        ALU.is_equal).then_inc(hit_ready, 1)

            def mask(n, c):
                m = n * EC + c
                dve.wait_ge(relu_done, m + 1)
                dve.wait_ge(mask_done, past(m + 1))
                dve.wait_ge(squared, past(n * EC + max(c - 1, 0)))
                nc.vector.tensor_tensor(hid_m[c % 2], hid[c % 2], ps[:, 4, :], ALU.mult).then_inc(masked, 1)

            def times_u(n, c):
                m = n * EC + c
                dve.wait_ge(squared, past(m + 1))
                dve.wait_ge(u_done, m + 1)
                if c == 0:
                    dve.wait_ge(wd_done, past(n * 2))
                nc.vector.tensor_tensor(inter[:, c, :], hid_q[c % 2], ps[:, 1 + 2 * (c % 2), :],
                                        ALU.mult).then_inc(inter_ready, 1)

            def reduce_early(n, c, u):
                t = (n - EARLY) * EC + c
                dve.wait_ge(a_scored[u], t + 1)
                nc.vector.tensor_reduce(most[0][:, t, u:u + 1], ps[:, 6:8, :], AX.XY, ALU.max).then_inc(a_reduced[u], 1)

            STEPS = GT * 4 + 4

            def group(n, s, early):
                rotate(n, 0)
                rotate(n, 1)
                route(n)
                for c in range(EC):
                    if early:
                        reduce_early(n, c, 0)
                    if early and 0 < c < GT - 1:
                        rotate(n, c + 1)
                    if not early and c + 2 < GT:
                        rotate(n, c + 2)
                    mask(n, c)
                    if early:
                        reduce_early(n, c, 1)
                    times_u(n, c)

            assert count[0] == SETUP_STEPS
            with dve.Fori(0, EARLY // 2) as gp:
                base[0], count[0] = gp * (2 * STEPS) + SETUP_STEPS, 0
                for s in range(2):
                    group(gp * 2 + s, s, False)
                assert count[0] == 2 * STEPS
            base[0], count[0] = SETUP_STEPS + EARLY * STEPS, 0
            for n in range(EARLY, NG):
                group(n, n % 2, True)

            nc.vector.memset(mpart, 0.0)
            nc.vector.memset(spread[1], 1.0)

            def reduce(t, head_slot, tile):
                for u in range(2):
                    dve.wait_ge(a_scored[u], t + 1)
                    nc.vector.tensor_reduce(most[head_slot][:, tile, u:u + 1], ps[:, 2 + 2 * u:4 + 2 * u, :], AX.XY,
                                            ALU.max).then_inc(a_reduced[u], 1)

            def cut_maxima(k, head, head_slot):
                if k == 0:
                    for u in range(2):
                        dve.wait_ge(a_reduced[u], past(head * KB + KB))
                else:
                    dve.wait_ge(dve_step, base[0] + count[0])
                if k == 1:
                    dve.wait_ge(mt_done, head)
                ins = (lambda: nc.vector.tensor_reduce(negm, most[head_slot], AX.X, ALU.max, negate=True),
                       lambda: nc.vector.tensor_copy(mpart[:, 0:KB], negm),
                       lambda: nc.vector.tensor_tensor(mres, negm, mpart[:, 0:KB], ALU.subtract),
                       lambda: nc.vector.tensor_copy(mpart[:, KB:2 * KB], mres),
                       lambda: nc.vector.tensor_tensor(mpart[:, 2 * KB:3 * KB], mres, mpart[:, KB:2 * KB],
                                                       ALU.subtract))[k]()
                if k < CUTS - 1:
                    count[0] += 1
                    ins.then_inc(dve_step, 1)
                else:
                    ins.then_inc(mpart_ready, 1)

            def copy_maxima(head, bank, slot_before=None, uses=None):
                dve.wait_ge(mt_done, head + 1)
                if uses is not None:
                    dve.wait_ge(shift_loaded[slot_before], uses)
                nc.vector.tensor_copy(mrow[0:NPART * KB, :], bank_b(bank)[0:NPART * KB, 0:P]).then_inc(mrow_ready, 1)

            base[0], count[0] = SETUP_STEPS + NG * STEPS, 0
            for k in range(CUTS):
                cut_maxima(k, 0, 0)
            copy_maxima(0, 5)
            for t in range(KB, AHEAD):
                reduce(t, t // KB, t % KB)
            assert count[0] == 4

            def invert(s, n):
                dve.wait_ge(spread_in[s], past(n * 16))
                nc.vector.reciprocal(spread[s], spread[s]).then_inc(rec_ready[s], 1)

            def step(pi, last_pair, s, kb):
                g = pi * (2 * KB) + (s * KB + kb)
                ahead = kb + AHEAD - KB
                coming = not (last_pair and s == 1)
                if kb == 4:
                    invert(1 - s, pi + s)
                if ahead == KB + COPY_STEP and coming:
                    copy_maxima(pi * 2 + (s + 1), 6 + (1 - s), s, (pi + 1) * 16)
                if not last_pair or (s == 0 and ahead < KB):
                    reduce(g + AHEAD, (s + 1 + ahead // KB) % 2, ahead % KB)
                k = ahead - (KB - 1)
                if 0 <= k <= CUTS // 2 and coming:
                    for i in range(2 * k, min(2 * k + 2, CUTS)):
                        cut_maxima(i, pi * 2 + (s + 1), 1 - s)

            def copy_sums(pi, s):
                dve.wait_ge(pv_done[1], past(pi * KB + (s + 1) * NB2))
                dve.wait_ge(spread_in[s], past(pi * 16))
                dve.wait_ge(o_stored[s], past(pi * (16 * QT)))
                nc.vector.tensor_copy(osb[s], ps[:, 6 + s, :]).then_inc(o_out[s], 1)

            def pair(pi, last_pair):
                for kb in range(1, KB):
                    step(pi, last_pair, 0, kb)
                step(pi, last_pair, 1, 0)
                copy_sums(pi, 0)
                for kb in range(1, KB):
                    step(pi, last_pair, 1, kb)
                if not last_pair:
                    step(pi + 1, False, 0, 0)
                copy_sums(pi, 1)

            step(0, False, 0, 0)
            with dve.Fori(0, NP - 1) as pi:
                base[0], count[0] = pi * 8 + (SETUP_STEPS + NG * STEPS + 4), 0
                pair(pi, False)
                assert count[0] == 8
            base[0], count[0] = (NP - 1) * 8 + (SETUP_STEPS + NG * STEPS + 4), 0
            pair(NP - 1, True)

            invert(1, NP)
            base[0], count[0] = base[0] + count[0], 0
            for b in range(B):
                for i in range(ENDT):
                    n = b * ENDT + i
                    if n == ENDT - 2:
                        dve.wait_ge(chunk_loaded, 16 * 2 * (NC + 1))
                        for t in range(QT):
                            sl = onum[:, NC - 1, t * W:(t + 1) * W]
                            nc.vector.tensor_tensor(sl, sl, orec[:, t * W:(t + 1) * W], ALU.mult).then_inc(normed, 1)
                    dve.wait_ge(proj_done, n + 1)
                    if n >= NR:
                        dve.wait_ge(res_stored[n % NR], 16 * (n // NR))
                    link(nc.vector.tensor_tensor(res[n % NR], ps[:, n % 4, :].rearrange("p (t d) -> p t d", d=D),
                                                 gate[:, 2 * n:2 * n + 2, :], ALU.mult))
                    nc.vector.tensor_tensor(res[n % NR], res[n % NR], x_sb[:, 2 * n:2 * n + 2, :],
                                            ALU.add).then_inc(res_ready[n % NR], 1)

        @block.gpsimd
        def _(pool):
            for counter in from_one:
                pool.sem_inc(counter, 1)
            pool.sem_inc(counters_set, 1)
            def center(n, s):
                pool.wait_ge(xt_done, n * 2 - 2)
                t = bass.ds(n * GT, GT)
                nc.gpsimd.tensor_tensor(xn[s], x_sb[:, t, :], mean[:, t].unsqueeze(2).to_broadcast([P, GT, D]),
                                        ALU.subtract).then_inc(centered, 1)

            def scale(n, s):
                pool.wait_ge(centered, n)
                nc.gpsimd.tensor_tensor(xn[s], xn[s], rstd[:, bass.ds(n * GT, GT)].unsqueeze(2).to_broadcast([P, GT, D]),
                                        ALU.mult).then_inc(xn_ready, 1)

            def low_part(n, j):
                pool.wait_ge(mid_ready, past(n * GT + (j + 1)))
                nc.gpsimd.tensor_tensor(parts[j % 2][:, 2, :], ra[j % 2], parts[j % 2][:, 1, :],
                                        ALU.subtract).then_inc(rope_done, 1)

            def group(n, s, has_next):
                for j in range(GT):
                    low_part(n, j)
                    if has_next and j == 1:
                        center(n + 1, 1 - s)
                    if has_next and j == 2:
                        scale(n + 1, 1 - s)

            with pool.Fori(0, NG // 2 - 1) as gp:
                for s in range(2):
                    group(gp * 2 + s, s, True)
            group(NG - 2, 0, True)
            group(NG - 1, 1, False)

            def stage(b, j, s, pi):
                pool.wait_ge(o_out[s], past(pi))
                h = j * 2 + s
                pool.wait_ge(consts_ready, 3)
                nc.gpsimd.tensor_copy(vst[s][:, :, 1:1 + DH],
                                      v_sb[:, b * KB:(b + 1) * KB, bass.ds(h * DH, DH)]).then_inc(v_staged[s], 1)

            def weigh(m):
                pool.wait_ge(chunk_loaded, 16 * 2 * (m + 1))
                nc.gpsimd.tensor_tensor(onum[:, m, :], onum[:, m, :], orec, ALU.mult).then_inc(chunk_weighed, 1)

            pool.wait_ge(parts_stored, past(PSTORES * NG))
            pool.wait_ge(gate_ready, past(2 * NG))
            nc.gpsimd.memset(kst[1][96:KS, :], 1.0).then_inc(consts_ready, 1)
            for s in range(2):
                pool.wait_ge(consts_ready, 1 + s)
                nc.gpsimd.memset(vst[s], 1.0).then_inc(consts_ready, 1)
            for m in range(NC):
                b, first = divmod(m * CP, H // 2)
                with pool.Fori(first, first + CP) as j:
                    for s in range(2):
                        stage(b, j, s, j + b * (H // 2))
                if m:
                    weigh(m - 1)
        @block.tensor
        def _(pe):
            pe.wait_ge(counters_set, 1)
            pe.wait_ge(first_loaded, 16 * 2)

            def transpose_x(n, s):
                pe.wait_ge(xn_ready, n + 1)
                for j in range(GT):
                    for k in range(KC):
                        last = nc.tensor.transpose(ps[:, j // 2, (2 * k + j % 2) * P:(2 * k + j % 2 + 1) * P],
                                                   xn[s][:, j, k * P:(k + 1) * P], ident[:])
                    if j % 2:
                        last.then_inc(xt_done, 1)

            def transpose_maxima(head, bank):
                pe.wait_ge(mpart_ready, head + 1)
                nc.tensor.transpose(bank_b(bank)[:, 0:P], mpart, ident_b[:]).then_inc(mt_done, 1)

            def score_early(n, c, u):
                t = (n - EARLY) * EC + c
                if u:
                    pe.wait_ge(a_reduced[0], past(t + 1))
                elif t:
                    pe.wait_ge(a_reduced[1], past(t))
                for h in range(2):
                    last = nc.tensor.matmul(ps[:, 6 + h, :], qa[0][0:KR, t * P:(t + 1) * P],
                                            ka[0][0:KR, (2 * u + h) * W:(2 * u + h + 1) * W], start=True, stop=True)
                last.then_inc(a_scored[u], 1)

            def group(n, s, has_next, early):
                pe.wait_ge(xt_out, n * 2 + 2)
                for j in range(GT):
                    o = 2 * (j % 2)
                    if j < 2:
                        pe.wait_ge(inter_ready, past(n * EC))
                    else:
                        pe.wait_ge(qkv_out, past(n * GT + j - 1))
                    for k in range(KC):
                        xt = xnT[s][:, k, j * P:(j + 1) * P]
                        nc.tensor.matmul(ps[:, o, :], xt, w_sb[:, k, 0:QK], start=(k == 0), stop=(k == KC - 1))
                        last = nc.tensor.matmul(ps[:, o + 1, 0:VG], xt, w_sb[:, k, QK:QK + VG],
                                                start=(k == 0), stop=(k == KC - 1))
                    last.then_inc(qkv_done, 1)
                pe.wait_ge(identity_ready, 1)
                pe.wait_ge(weights_loaded, 16 * NW)
                if early:
                    pe.wait_ge(gate_ready, past(n * 2))
                    if n == EARLY:
                        pe.wait_ge(a_loaded[0], 16 * LOADS)
                for c in range(EC):
                    m = n * EC + c
                    o = 2 * (c % 2)
                    if c < 2:
                        pe.wait_ge(qkv_out, past(n * GT + (c + 3)))
                    else:
                        pe.wait_ge(inter_ready, past(m - 1))
                    for k in range(KC):
                        last = nc.tensor.matmul(ps[:, o, :], wg_sb[:, k, c * P:(c + 1) * P], xnT[s][:, k, :],
                                                start=(k == 0), stop=(k == KC - 1))
                    last.then_inc(g_done, 1)
                    for i in range(2):
                        if i == 1:
                            for k in range(KC):
                                last = nc.tensor.matmul(ps[:, o + 1, :], wu_sb[:, k, c * P:(c + 1) * P],
                                                        xnT[s][:, k, :], start=(k == 0), stop=(k == KC - 1))
                            last.then_inc(u_done, 1)
                        if early:
                            score_early(n, c, i)
                        if i == 0:
                            pe.wait_ge(rope_done, past(m + 1))
                        pe.wait_ge(pt_out, past(m * 2 + i))
                        for q in range(HM):
                            a, kc = divmod(i * HM + q, 2 * KC)
                            last = nc.tensor.transpose(bank_b(5)[:, q * P:(q + 1) * P],
                                                       parts[c % 2][:, a, kc * P:(kc + 1) * P], ident_b[:])
                        last.then_inc(pt_done, 1)
                    if c == 0:
                        pe.wait_ge(hit_ready, past(n + 1))
                    pe.wait_ge(masked, past(m))
                    for j in range(GT):
                        for e in range(EP):
                            last = nc.tensor.matmul(ps[e * DE:(e + 1) * DE, 4, j * P:(j + 1) * P],
                                                    won[:, j, EP * c + e:EP * c + e + 1].to_broadcast([P, DE]),
                                                    ident_b[:], start=True, stop=True)
                    last.then_inc(mask_done, 1)
                if has_next:
                    pe.wait_ge(inter_ready, past(n * EC + (EC - 1)))
                    transpose_x(n + 1, 1 - s)
                pe.wait_ge(inter_ready, past(n * EC + EC))
                pe.wait_ge(gate_ready, past(n * 2))
                if early:
                    pe.wait_ge(a_reduced[1], past((n - EARLY) * EC + EC))
                for j in range(GT):
                    for c in range(EC):
                        last = nc.tensor.matmul(ps[:, 6 + j // 2, (j % 2) * D:(j % 2 + 1) * D],
                                                inter[:, c, j * P:(j + 1) * P], wd_sb[:, c, :],
                                                start=(c == 0), stop=(c == EC - 1))
                    if j % 2:
                        last.then_inc(wd_done, 1)
                    if j == 1 and not has_next:
                        pe.wait_ge(pt_out, past(2 * NT))
                        transpose_maxima(0, 5)

            transpose_x(0, 0)
            with pe.Fori(0, EARLY // 2) as gp:
                for s in range(2):
                    group(gp * 2 + s, s, True, False)
            for n in range(EARLY, NG):
                group(n, n % 2, n < NG - 1, True)

            def score_a(t, head_slot, tile, u):
                pe.wait_ge(a_reduced[u], past(t))
                for c in range(2):
                    last = nc.tensor.matmul(ps[:, 2 + 2 * u + c, :], qa[head_slot][0:KR, tile * P:(tile + 1) * P],
                                            ka[head_slot][0:KR, (2 * u + c) * W:(2 * u + c + 1) * W],
                                            start=True, stop=True)
                last.then_inc(a_scored[u], 1)

            def score(s, kb, c, n):
                pe.wait_ge(exp_done[c % 2], past(n))
                nc.tensor.matmul(ps[:, c % 2, :], kst[s][0:KS, kb * P:(kb + 1) * P],
                                 qst[s][0:KS, c * W:(c + 1) * W], start=True, stop=True).then_inc(scored[c % 2], 1)

            pe.wait_ge(a_loaded[1], 16 * LOADS)
            pe.wait_ge(mrow_ready, 1)
            for t in range(KB, AHEAD):
                for u in range(2):
                    score_a(t, t // KB, t % KB, u)
            pe.wait_ge(loaded[0], 16 * LOADS)
            pe.wait_ge(shift_loaded[0], 16)
            pe.wait_ge(gate_ready, past(2 * NG))
            for c in range(QT):
                score(0, 0, c, c // 2)

            def pair(pi, last_pair):
                for s in range(2):
                    for kb in range(KB):
                        g = pi * (2 * KB) + (s * KB + kb)
                        ahead = kb + AHEAD - KB
                        with_a = not last_pair or (s == 0 and ahead < KB)
                        with_b = not (last_pair and s == 1 and kb == KB - 1)
                        a_slot = (s + 1 + ahead // KB) % 2
                        b_slot = s if kb < KB - 1 else 1 - s
                        used = pi * (4 * KB) + (s * 2 * KB + kb * 2 + 2)
                        if kb == KB - 1 and with_b:
                            pe.wait_ge(loaded[b_slot], (pi + 1 + s) * (16 * LOADS))
                            pe.wait_ge(shift_loaded[b_slot], (pi + 1 + s) * 16)
                        if with_a and ahead % KB == 0:
                            pe.wait_ge(a_loaded[a_slot], (pi + 2) * (16 * LOADS))
                        if with_b:
                            for c in range(2):
                                score(b_slot, (kb + 1) % KB, c, used)
                        if with_a:
                            for u in range(2):
                                score_a(g + AHEAD, a_slot, ahead % KB, u)
                        if with_b:
                            for c in range(2, QT):
                                score(b_slot, (kb + 1) % KB, c, used + 1)
                        if ahead == KB + COPY_STEP - 1 and not (last_pair and s == 1):
                            transpose_maxima(pi * 2 + (s + 1), 6 + (1 - s))
                        if kb == 0:
                            pe.wait_ge(v_staged[s], pi + 1)
                            pe.wait_ge(o_out[s], past(pi))
                            pe.wait_ge(mrow_ready, pi * 2 + (s + 1))
                        for i in range(2):
                            pe.wait_ge(exp_done[i], past(used))
                        for c in range(QT):
                            last = nc.tensor.matmul(ps[32 * c:32 * (c + 1), 6 + s, :], vst[s][:, kb, :],
                                                    prob[kb % 2][:, c * W:(c + 1) * W],
                                                    start=(kb == 0), stop=(kb == KB - 1))
                        last.then_inc(pv_done[kb % 2], 1)

            with pe.Fori(0, NP - 1) as pi:
                pair(pi, False)
            pair(NP - 1, True)

            for b in range(B):
                for i in range(ENDT):
                    n = b * ENDT + i
                    if i == 0:
                        pe.wait_ge(chunk_weighed, min(KC * (b + 1), NC - 1))
                        pe.wait_ge(a_reduced[0], past(NH * KB))
                    if b == B - 1:
                        pe.wait_ge(normed, i // 2 + 1)
                    if n >= 4:
                        pe.wait_ge(res_ready[n % 4], n // 4)
                    for t in range(2):
                        for k in range(KC):
                            last = nc.tensor.matmul(ps[:, i % 4, t * D:(t + 1) * D],
                                                    onum[:, b * KC + k, (2 * i + t) * P:(2 * i + t + 1) * P], wo_sb[:, k, :],
                                                    start=(k == 0), stop=(k == KC - 1))
                    last.then_inc(proj_done, 1)


def kernel(L0_attn_x, L0_attn_w_qkv, L0_attn_w_out, L0_ffn_gate_w, L0_ffn_wg, L0_ffn_wu, L0_ffn_wd):
    import numpy as np
    import concourse.bacc as bacc
    from concourse import mybir
    from concourse.bass_utils import run_bass_kernel_spmd

    def rows(a):
        return np.ascontiguousarray(a.reshape(-1, 128, a.shape[-1]).transpose(1, 0, 2))

    x = np.ascontiguousarray(L0_attn_x)
    e, d, f = L0_ffn_wg.shape
    length, half = x.shape[1], 8
    inv = np.float32(1.0) / np.float32(10000.0) ** (np.arange(half, dtype=np.float32) / np.float32(half))
    ang = np.arange(length, dtype=np.float32)[:, None] * inv[None, :].astype(np.float32)
    table = np.concatenate([np.cos(ang), np.sin(ang), -np.sin(ang)], axis=-1).astype(np.float32)
    arrays = {
        "x": x,
        "w": rows(np.concatenate([np.asarray(L0_attn_w_qkv), np.asarray(L0_ffn_gate_w)], axis=0).T),
        "wout": rows(np.asarray(L0_attn_w_out).T),
        "wg": rows(np.asarray(L0_ffn_wg).transpose(1, 0, 2).reshape(d, e * f)),
        "wu": rows(np.asarray(L0_ffn_wu).transpose(1, 0, 2).reshape(d, e * f)),
        "wd": rows(np.asarray(L0_ffn_wd).reshape(e * f, d)),
        "rope": np.tile(rows(table), (1, x.shape[0], 1)),
        "ident": np.eye(128, dtype=np.float32),
        "rank": np.tile(np.arange(e, 0, -1, dtype=np.float32), (128, 1)),
    }
    nc = bacc.Bacc("TRN2", target_bir_lowering=False, num_devices=1)
    args, feed = [], {}
    for name, a in arrays.items():
        feed[f"in_{name}"] = a
        args.append(nc.dram_tensor(f"in_{name}", a.shape, mybir.dt.from_np(a.dtype), kind="ExternalInput").ap())
    args.append(nc.dram_tensor("out", x.shape, mybir.dt.float32, kind="ExternalOutput").ap())
    layer_kernel(nc, *args)
    got = run_bass_kernel_spmd(nc, [feed], core_ids=[0])
    return got.results[0]["out"]
```
